# Optimizing a Trainium2 kernel written in Bass

```python
import numpy as np
import jax
import jax.numpy as jnp

def _softmax(x, axis=-1):
    return jax.nn.softmax(x, axis=axis)

def _gelu(x):
    return jax.nn.gelu(x, approximate=True)

def _silu(x):
    return jax.nn.silu(x)

def _sigmoid(x):
    return jax.nn.sigmoid(x)

def _layernorm(x, axis=-1, eps=1e-05):
    m = jnp.mean(x, axis=axis, keepdims=True)
    v = jnp.var(x, axis=axis, keepdims=True)
    return (x - m) / jnp.sqrt(v + eps)

def _scatter_add(tgt, idx, src, axis=0):
    return tgt.at[idx].add(src)

def _segment_sum(src, seg, n):
    return jax.ops.segment_sum(src, seg, n)
kernel_name = 'mk_flamingo_gated_d2_seqx_r8_03a0f1'

def setup_inputs(seed: int=0):
    np.random.seed(seed)
    _w = jnp.asarray

    def _rec_inputs():
        import jax
        import jax.numpy as jnp
        _rk = jax.random.key(seed)
        x = 7.22e-05 + 1 * jax.random.normal(jax.random.fold_in(_rk, 1), (8, 128, 512), jnp.float32)
        _lenS = 128 - jax.random.randint(jax.random.fold_in(_rk, 7), (8,), 0, max(1, 128 // 4) + 1, jnp.int32)
        _lenS2 = 128 - jax.random.randint(jax.random.fold_in(_rk, 8), (8,), 0, max(1, 128 // 4) + 1, jnp.int32)
        _ctx_4096P = jax.random.normal(jax.random.fold_in(_rk, 11), (8, 16, 512), jnp.float32)
        _ctx_4096c = jax.random.dirichlet(jax.random.fold_in(_rk, 511), 0.3 * jnp.ones((16,), jnp.float32), (8, 128))
        _ctx_4096t = jnp.einsum('bsk,bkd->bsd', _ctx_4096c, _ctx_4096P)
        _ctx_4096t = _ctx_4096t * jax.lax.rsqrt(jnp.mean(jnp.square(_ctx_4096t)) + 1e-12) * 0.953939
        ctx_4096 = 4.13588e-05 + 0.999923 * (_ctx_4096t + 0.3 * jax.random.normal(jax.random.fold_in(_rk, 611), (8, 128, 512), jnp.float32))
        _validS = jnp.arange(128)[None, :] < _lenS[:, None]
        _validS2 = jnp.arange(128)[None, :] < _lenS2[:, None]
        _causal = jnp.tril(jnp.ones((128, 128), dtype=bool))
        mask_BxSxS2_bk0 = jnp.logical_not(jnp.broadcast_to(_validS2[:, None, :], (8, 128, 128)))
        _g = jax.random.normal(jax.random.fold_in(_rk, 9001), (2, 2), jnp.float32)
        _g = jnp.sign(_g) * jnp.maximum(jnp.abs(_g), 1.0) + (_g == 0) * 1.0
        g_xattn = _g[0]
        g_ffn = _g[1]
        return (x, ctx_4096, mask_BxSxS2_bk0, g_xattn, g_ffn)
    x, ctx_4096, mask_BxSxS2_bk0, g_xattn, g_ffn = _rec_inputs()

    def _L0_xattn_setup():
        import jax, jax.numpy as jnp
        import numpy as np
        B, LQ, LK, D, H, DH = (2, 128, 128, 512, 32, 128)
        EPS = 1e-05

        def _rmsnorm(x, weight):
            var = jnp.mean(jnp.square(x), axis=-1, keepdims=True)
            return x * jax.lax.rsqrt(var + EPS) * weight
        key = jax.random.key(seed)
        ks = jax.random.split(key, 8)
        scale = 0.02
        return {'hidden_states': jax.random.normal(ks[0], (B, LQ, D), jnp.float32), 'key_value_states': jax.random.normal(ks[1], (B, LK, D), jnp.float32), 'attention_mask': jax.random.randint(ks[2], (B, LQ, LK), 0, 2) > 0, 'position_bias': jax.random.normal(ks[3], (H, LQ, LK), jnp.float32), 'ln_weight': jnp.ones((D,), jnp.float32), 'w_q': jax.random.normal(ks[4], (H * DH, D), jnp.float32) * scale, 'w_k': jax.random.normal(ks[5], (H * DH, D), jnp.float32) * scale, 'w_v': jax.random.normal(ks[6], (H * DH, D), jnp.float32) * scale, 'w_out': jax.random.normal(ks[7], (D, H * DH), jnp.float32) * scale}
    _L0_xattn_all = _L0_xattn_setup()
    _L0_xattn_in = {k: v for k, v in _L0_xattn_all.items() if k in ('position_bias', 'ln_weight', 'w_q', 'w_k', 'w_v', 'w_out')}
    del _L0_xattn_all

    def _L0_ffn_setup():
        import jax, jax.numpy as jnp
        import numpy as np
        NF4_CODE = jnp.array([-1.0, -0.6961928009986877, -0.5250730514526367, -0.39491748809814453, -0.28444138169288635, -0.18477343022823334, -0.09105003625154495, 0.0, 0.07958029955625534, 0.16093020141124725, 0.24611230194568634, 0.33791524171829224, 0.44070982933044434, 0.5626170039176941, 0.7229568362236023, 1.0], dtype=jnp.float32)
        BLOCKSIZE = 64

        def nf4_quant_dequant(w):
            shape = w.shape
            flat = w.reshape(-1, BLOCKSIZE)
            absmax = jnp.max(jnp.abs(flat), axis=1, keepdims=True)
            normalized = flat / jnp.where(absmax == 0, 1.0, absmax)
            bounds = (NF4_CODE[:-1] + NF4_CODE[1:]) * 0.5
            idx = jnp.searchsorted(bounds, normalized)
            return (NF4_CODE[idx] * absmax).reshape(shape)
        key = jax.random.key(seed)
        k1, k2, k3, kx = jax.random.split(key, 4)
        D, H = (512, 1376)
        scale = 0.02
        w1 = jax.random.normal(k1, (H, D), jnp.float32) * scale
        w2 = jax.random.normal(k2, (H, D), jnp.float32) * scale
        w3 = jax.random.normal(k3, (D, H), jnp.float32) * scale
        x = jax.random.normal(kx, (2, 256, D), jnp.float32)
        return {'x': x, 'w1': w1, 'w2': w2, 'w3': w3}
    _L0_ffn_all = _L0_ffn_setup()
    _L0_ffn_in = {k: v for k, v in _L0_ffn_all.items() if k in ('w1', 'w2', 'w3')}
    del _L0_ffn_all

    def _L1_xattn_setup():
        import jax, jax.numpy as jnp
        import numpy as np
        DIM = 512
        NUM_HEADS = 32
        NUM_KV_HEADS = 8
        HEAD_DIM = DIM // NUM_HEADS
        KV_DIM = DIM // (NUM_HEADS // NUM_KV_HEADS)
        B, S = (1, 256)
        key = jax.random.key(seed)
        ks = jax.random.split(key, 7)
        w_scale = DIM ** (-0.5)
        return {'query': jax.random.normal(ks[0], (B, S, DIM), jnp.float32), 'key': jax.random.normal(ks[1], (B, S, DIM), jnp.float32), 'value': jax.random.normal(ks[2], (B, S, DIM), jnp.float32), 'Wq': jax.random.normal(ks[3], (DIM, DIM), jnp.float32) * w_scale, 'Wk': jax.random.normal(ks[4], (DIM, KV_DIM), jnp.float32) * w_scale, 'Wv': jax.random.normal(ks[5], (DIM, KV_DIM), jnp.float32) * w_scale, 'Wo': jax.random.normal(ks[6], (DIM, DIM), jnp.float32) * w_scale}
    _L1_xattn_all = _L1_xattn_setup()
    _L1_xattn_in = {k: v for k, v in _L1_xattn_all.items() if k in ('Wq', 'Wk', 'Wv', 'Wo')}
    del _L1_xattn_all

    def _L1_ffn_setup():
        import jax, jax.numpy as jnp
        import numpy as np
        HIDDEN = 512
        INTER = 1376
        GROUPSIZE = 128
        PACK = 8

        def dequant_gptq(qweight, scales, zeros, groupsize):
            K = qweight.shape[0] * PACK
            N = qweight.shape[1]
            k = jnp.arange(K)
            q = qweight[k // PACK, :] >> (k % PACK * 4)[:, None] & 15
            n = jnp.arange(N)
            z = zeros[:, n // PACK] >> (n % PACK * 4)[None, :] & 15
            s = scales.astype(jnp.float32)
            zp = (z.astype(jnp.float32) + 1.0) * s
            g = k // groupsize
            return q.astype(jnp.float32) * s[g] - zp[g]
        key = jax.random.key(seed)
        ks = jax.random.split(key, 11)
        imax = 2147483647
        G_h = HIDDEN // GROUPSIZE
        G_i = (INTER + GROUPSIZE - 1) // GROUPSIZE
        x = (jax.random.normal(ks[0], (2, 256, HIDDEN), dtype=jnp.float32) * 0.5).astype(jnp.float16)
        return {'x': x, 'gate_qweight': jax.random.randint(ks[1], (HIDDEN // PACK, INTER), 0, imax, dtype=jnp.int32), 'gate_scales': (jax.random.uniform(ks[2], (G_h, INTER), dtype=jnp.float32) * 0.01 + 0.001).astype(jnp.float16), 'gate_zeros': jax.random.randint(ks[3], (G_h, INTER // PACK), 0, imax, dtype=jnp.int32), 'up_qweight': jax.random.randint(ks[4], (HIDDEN // PACK, INTER), 0, imax, dtype=jnp.int32), 'up_scales': (jax.random.uniform(ks[5], (G_h, INTER), dtype=jnp.float32) * 0.01 + 0.001).astype(jnp.float16), 'up_zeros': jax.random.randint(ks[6], (G_h, INTER // PACK), 0, imax, dtype=jnp.int32), 'down_qweight': jax.random.randint(ks[7], (INTER // PACK, HIDDEN), 0, imax, dtype=jnp.int32), 'down_scales': (jax.random.uniform(ks[8], (G_i, HIDDEN), dtype=jnp.float32) * 0.01 + 0.001).astype(jnp.float16), 'down_zeros': jax.random.randint(ks[9], (G_i, HIDDEN // PACK), 0, imax, dtype=jnp.int32)}
    _L1_ffn_all = _L1_ffn_setup()
    _L1_ffn_in = {k: v for k, v in _L1_ffn_all.items() if k in ('gate_qweight', 'gate_scales', 'gate_zeros', 'up_qweight', 'up_scales', 'up_zeros', 'down_qweight', 'down_scales', 'down_zeros')}
    del _L1_ffn_all
    return {'x': x, 'ctx_4096': ctx_4096, 'mask_BxSxS2_bk0': mask_BxSxS2_bk0, 'g_xattn': g_xattn, 'g_ffn': g_ffn, 'L0_xattn_position_bias': _L0_xattn_in['position_bias'], 'L0_xattn_ln_weight': _L0_xattn_in['ln_weight'], 'L0_xattn_w_q': _L0_xattn_in['w_q'], 'L0_xattn_w_k': _L0_xattn_in['w_k'], 'L0_xattn_w_v': _L0_xattn_in['w_v'], 'L0_xattn_w_out': _L0_xattn_in['w_out'], 'L0_ffn_w1': _L0_ffn_in['w1'], 'L0_ffn_w2': _L0_ffn_in['w2'], 'L0_ffn_w3': _L0_ffn_in['w3'], 'L1_xattn_Wq': _L1_xattn_in['Wq'], 'L1_xattn_Wk': _L1_xattn_in['Wk'], 'L1_xattn_Wv': _L1_xattn_in['Wv'], 'L1_xattn_Wo': _L1_xattn_in['Wo'], 'L1_ffn_gate_qweight': _L1_ffn_in['gate_qweight'], 'L1_ffn_gate_scales': _L1_ffn_in['gate_scales'], 'L1_ffn_gate_zeros': _L1_ffn_in['gate_zeros'], 'L1_ffn_up_qweight': _L1_ffn_in['up_qweight'], 'L1_ffn_up_scales': _L1_ffn_in['up_scales'], 'L1_ffn_up_zeros': _L1_ffn_in['up_zeros'], 'L1_ffn_down_qweight': _L1_ffn_in['down_qweight'], 'L1_ffn_down_scales': _L1_ffn_in['down_scales'], 'L1_ffn_down_zeros': _L1_ffn_in['down_zeros']}

def reference(x, ctx_4096, mask_BxSxS2_bk0, g_xattn, g_ffn, L0_xattn_position_bias, L0_xattn_ln_weight, L0_xattn_w_q, L0_xattn_w_k, L0_xattn_w_v, L0_xattn_w_out, L0_ffn_w1, L0_ffn_w2, L0_ffn_w3, L1_xattn_Wq, L1_xattn_Wk, L1_xattn_Wv, L1_xattn_Wo, L1_ffn_gate_qweight, L1_ffn_gate_scales, L1_ffn_gate_zeros, L1_ffn_up_qweight, L1_ffn_up_scales, L1_ffn_up_zeros, L1_ffn_down_qweight, L1_ffn_down_scales, L1_ffn_down_zeros):
    import jax
    import jax.numpy as jnp

    def _L0_xattn_ref(hidden_states, key_value_states, attention_mask, position_bias, ln_weight, w_q, w_k, w_v, w_out):
        import jax, jax.numpy as jnp
        import numpy as np
        B, LQ, LK, D, H, DH = (2, 128, 128, 512, 32, 128)
        EPS = 1e-05

        def _rmsnorm(x, weight):
            var = jnp.mean(jnp.square(x), axis=-1, keepdims=True)
            return x * jax.lax.rsqrt(var + EPS) * weight
        x = _rmsnorm(hidden_states, ln_weight)
        b, lq, _ = x.shape
        lk = key_value_states.shape[1]
        h_q = (x @ w_q.T).reshape(b, lq, H, DH)
        h_k = (key_value_states @ w_k.T).reshape(b, lk, H, DH)
        h_v = (key_value_states @ w_v.T).reshape(b, lk, H, DH)
        score = jnp.einsum('bqhd,bkhd->bhqk', h_q, h_k)
        score = score + position_bias[None]
        m = attention_mask[:, None]
        score = jnp.where(m, score, -jnp.inf)
        score = jax.nn.softmax(score, axis=-1)
        score = jnp.where(m, score, 0.0)
        attn = jnp.einsum('bhqk,bkhd->bqhd', score, h_v).reshape(b, lq, H * DH)
        out = attn @ w_out.T
        return hidden_states + out

    def _L0_ffn_ref(x, w1, w2, w3):
        import jax, jax.numpy as jnp
        import numpy as np
        NF4_CODE = jnp.array([-1.0, -0.6961928009986877, -0.5250730514526367, -0.39491748809814453, -0.28444138169288635, -0.18477343022823334, -0.09105003625154495, 0.0, 0.07958029955625534, 0.16093020141124725, 0.24611230194568634, 0.33791524171829224, 0.44070982933044434, 0.5626170039176941, 0.7229568362236023, 1.0], dtype=jnp.float32)
        BLOCKSIZE = 64

        def nf4_quant_dequant(w):
            shape = w.shape
            flat = w.reshape(-1, BLOCKSIZE)
            absmax = jnp.max(jnp.abs(flat), axis=1, keepdims=True)
            normalized = flat / jnp.where(absmax == 0, 1.0, absmax)
            bounds = (NF4_CODE[:-1] + NF4_CODE[1:]) * 0.5
            idx = jnp.searchsorted(bounds, normalized)
            return (NF4_CODE[idx] * absmax).reshape(shape)
        dq1 = nf4_quant_dequant(w1)
        dq2 = nf4_quant_dequant(w2)
        dq3 = nf4_quant_dequant(w3)
        gate = jnp.einsum('bsd,hd->bsh', x, dq1)
        up = jnp.einsum('bsd,hd->bsh', x, dq2)
        h = jax.nn.silu(gate) * up
        return jnp.einsum('bsh,dh->bsd', h, dq3)

    def _L1_xattn_ref(query, key, value, Wq, Wk, Wv, Wo):
        import jax, jax.numpy as jnp
        import numpy as np
        DIM = 512
        NUM_HEADS = 32
        NUM_KV_HEADS = 8
        HEAD_DIM = DIM // NUM_HEADS
        KV_DIM = DIM // (NUM_HEADS // NUM_KV_HEADS)
        B, S = (1, 256)
        b, sq, _ = query.shape
        _, sk, _ = key.shape
        rep = NUM_HEADS // NUM_KV_HEADS
        q = (query @ Wq).reshape(b, sq, NUM_HEADS, HEAD_DIM).transpose(0, 2, 1, 3)
        k = (key @ Wk).reshape(b, sk, NUM_KV_HEADS, HEAD_DIM).transpose(0, 2, 1, 3)
        v = (value @ Wv).reshape(b, sk, NUM_KV_HEADS, HEAD_DIM).transpose(0, 2, 1, 3)
        k = jnp.repeat(k, rep, axis=1)
        v = jnp.repeat(v, rep, axis=1)
        scale = HEAD_DIM ** (-0.5)
        scores = jnp.einsum('bhqd,bhkd->bhqk', q, k) * scale
        probs = jax.nn.softmax(scores, axis=-1)
        out = jnp.einsum('bhqk,bhkd->bhqd', probs, v)
        out = out.transpose(0, 2, 1, 3).reshape(b, sq, DIM)
        return out @ Wo

    def _L1_ffn_ref(x, gate_qweight, gate_scales, gate_zeros, up_qweight, up_scales, up_zeros, down_qweight, down_scales, down_zeros):
        import jax, jax.numpy as jnp
        import numpy as np
        HIDDEN = 512
        INTER = 1376
        GROUPSIZE = 128
        PACK = 8

        def dequant_gptq(qweight, scales, zeros, groupsize):
            K = qweight.shape[0] * PACK
            N = qweight.shape[1]
            k = jnp.arange(K)
            q = qweight[k // PACK, :] >> (k % PACK * 4)[:, None] & 15
            n = jnp.arange(N)
            z = zeros[:, n // PACK] >> (n % PACK * 4)[None, :] & 15
            s = scales.astype(jnp.float32)
            zp = (z.astype(jnp.float32) + 1.0) * s
            g = k // groupsize
            return q.astype(jnp.float32) * s[g] - zp[g]
        B, S, H = x.shape
        x2 = x.reshape(-1, H).astype(jnp.float32)
        Wg = dequant_gptq(gate_qweight, gate_scales, gate_zeros, GROUPSIZE)
        Wu = dequant_gptq(up_qweight, up_scales, up_zeros, GROUPSIZE)
        Wd = dequant_gptq(down_qweight, down_scales, down_zeros, GROUPSIZE)
        gate = x2 @ Wg
        up = x2 @ Wu
        inter = gate * jax.nn.sigmoid(gate) * up
        out = (inter @ Wd).astype(jnp.float16)
        return out.reshape(B, S, H)
    x = x + jnp.tanh(g_xattn[0]) * _L0_xattn_ref(_layernorm(x, axis=-1), ctx_4096, mask_BxSxS2_bk0, L0_xattn_position_bias, L0_xattn_ln_weight, L0_xattn_w_q, L0_xattn_w_k, L0_xattn_w_v, L0_xattn_w_out)
    x = x + jnp.tanh(g_ffn[0]) * _L0_ffn_ref(_layernorm(x, axis=-1), L0_ffn_w1, L0_ffn_w2, L0_ffn_w3)
    x = x + jnp.tanh(g_xattn[1]) * _L1_xattn_ref(_layernorm(x, axis=-1), ctx_4096, ctx_4096, L1_xattn_Wq, L1_xattn_Wk, L1_xattn_Wv, L1_xattn_Wo)
    x = x + jnp.tanh(g_ffn[1]) * _L1_ffn_ref(_layernorm(x, axis=-1), L1_ffn_gate_qweight, L1_ffn_gate_scales, L1_ffn_gate_zeros, L1_ffn_up_qweight, L1_ffn_up_scales, L1_ffn_up_zeros, L1_ffn_down_qweight, L1_ffn_down_scales, L1_ffn_down_zeros)
    return x

_drawn_inputs = setup_inputs


def setup_inputs(seed=0):
    import zlib

    import numpy as np

    out = dict(_drawn_inputs(seed))
    spreads = {'g_ffn': (-1.0, 0.2), 'L0_xattn_ln_weight': (1.0, 0.2)}
    factors = {}
    for name, (base, spread) in spreads.items():
        noise = np.random.default_rng([zlib.crc32(name.encode()), seed]).standard_normal(out[name].shape)
        drawn = base * np.exp(spread * noise) if base else spread * noise
        out[name] = jnp.asarray(drawn.astype(out[name].dtype))
    for name, factor in factors.items():
        out[name] = (out[name] * factor).astype(out[name].dtype)
    return out
```

```python
from contextlib import ExitStack

import numpy as np

import concourse.bass as bass
from concourse import mybir

F32 = mybir.dt.float32
F32R = mybir.dt.float32r
BF16 = mybir.dt.bfloat16
F16 = mybir.dt.float16
I32 = mybir.dt.int32
U8 = mybir.dt.uint8
ALU = mybir.AluOpType
ACT = mybir.ActivationFunctionType
AX = mybir.AxisListType

P = 128
NB = 8
S = 128
TOK = NB * S
D = 512
KT = D // P
H0, DH0 = 32, 128
GH = 4
GROUPS = H0 // GH
HALF = 512
QUAD = HALF // S
H1, KV1, DH1 = 32, 8, 16
REP1 = H1 // KV1
FF = 1376
FT = -(-FF // P)
FPAD = FT * P
FREST = FF - (FT - 1) * P
EPS = 1e-5
MASKED = -1e30

NF4_CODE = np.array(
    [-1.0, -0.6961928009986877, -0.5250730514526367, -0.39491748809814453, -0.28444138169288635,
     -0.18477343022823334, -0.09105003625154495, 0.0, 0.07958029955625534, 0.16093020141124725,
     0.24611230194568634, 0.33791524171829224, 0.44070982933044434, 0.5626170039176941,
     0.7229568362236023, 1.0], dtype=np.float32)
NF4_BOUNDS = ((NF4_CODE[:-1] + NF4_CODE[1:]) * np.float32(0.5)).astype(np.float32)
NLEV = len(NF4_BOUNDS)
QB = 64
NFW = (2 * FPAD + FF) * D // P
NFC = 512
NFTAIL = NFW - H0 * NFC


def nth(per_group, g, n):
    assert -per_group <= n < per_group
    return g * per_group + (per_group + n + 1)


class Shared:
    pass


def flamingo(nc, x, ctx_in, mask, gains, lnw, pbias, wqk0, wv0, wo0, nf4_src, gq, gs, gz, nibble_shift, wkv1, wq1, wo1, out):
    stack = ExitStack()
    with stack:
        M = Shared()
        sb = lambda name, shape, dt, where=stack: where.enter_context(nc.sbuf_tensor(name, shape, dt))
        pb = lambda name: stack.enter_context(nc.psum_tensor(name, [P, HALF], F32))

        sems = []

        def sem(name):
            sems.append(nc.alloc_semaphore(name))
            return sems[-1]

        def phase(run, *args):
            run(nc, M, sb, sem, *args)

        M.acc = sb("acc", [P, NB, D], F32)
        M.xT_hi = sb("xT_hi", [P, KT, TOK], F32R)
        M.xT_lo = sb("xT_lo", [P, KT, TOK], F32R)
        M.ident = sb("ident", [P, P], F32)
        M.ident_b = sb("ident_b", [P, P], BF16)
        M.tg = sb("tg", [P, 4], F32)
        M.stats = sb("stats", [P, NB, 6], F32)
        M.mv = sb("mv", [P, NB, 2], F32)
        M.ve = sb("ve", [P, NB], F32)
        M.sd = sb("sd", [P, NB], F32)
        M.rs = sb("rs", [P, NB], F32)
        M.nt = sb("nt", [P, NB], F32)
        M.pj = [pb(f"pj{i}") for i in range(4)]
        M.sc = [pb(f"sc{i}") for i in range(2)]
        M.tp = [pb(f"tp{i}") for i in range(2)]
        M.v1 = sb("v1", [P, NB, KV1, DH1 + 1], F32)
        M.k1_dram = nc.dram_tensor("k1_dram", [2, KV1, 2, DH1, TOK], F32, kind="Internal").ap()
        M.nf4_dq = nc.dram_tensor("nf4_dq", [P, NFW], F32, kind="Internal").ap()

        with ExitStack() as with_context:
            M.cT_hi = sb("cT_hi", [P, KT, TOK], F32R, with_context)
            M.cT_lo = sb("cT_lo", [P, KT, TOK], F32R, with_context)
            M.maskneg = sb("maskneg", [P, TOK], BF16, with_context)
            M.rowany = sb("rowany", [P, NB], F32, with_context)
            phase(setup_phase, x, ctx_in, mask, gains, lnw, nf4_src, wkv1)
            phase(attention0_phase, pbias, wqk0, wv0, wo0, nf4_src)
        nc.clear_and_free_semaphores(sems)
        nc.all_engine_barrier()
        phase(ffn_phase, 0, None, None, None, None)
        phase(attention1_phase, wq1, wo1)
        phase(ffn_phase, 1, gq, gs, gz, nibble_shift)
        phase(output_phase, out)


def output_phase(nc, M, sb, sem, out):
    s_out = sem("s_out")
    with nc.Block() as block:
        @block.sync
        def _(sp):
            sp.dma_start(out.rearrange("b s d -> s b d"), M.acc[:, :, :]).then_inc(s_out, 16)
            sp.wait_ge(s_out, 16)


class RootSteps:

    def __init__(self, M, sem, tag):
        self.M = M
        self.asked = sem(f"s_{tag}_ve")
        self.rooted = sem(f"s_{tag}_root")
        self.step = sem(f"s_{tag}_newton")

    def scalar(self, act):
        act.wait_ge(self.asked, 1)
        act.activation(self.M.sd[:, :], self.M.ve[:, :], ACT.Sqrt).then_inc(self.rooted, 1)

    def vector(self, dve):
        M = self.M
        dve.wait_ge(self.rooted, 1)
        dve.reciprocal(M.rs[:, :], M.sd[:, :]).then_inc(self.step, 1)
        dve.wait_ge(self.step, 1)
        dve.tensor_tensor(M.nt[:, :], M.rs[:, :], M.rs[:, :], ALU.mult).then_inc(self.step, 1)
        dve.wait_ge(self.step, 2)
        dve.tensor_tensor(M.nt[:, :], M.nt[:, :], M.ve[:, :], ALU.mult).then_inc(self.step, 1)
        dve.wait_ge(self.step, 3)
        dve.tensor_scalar(M.nt[:, :], M.nt[:, :], -0.5, 1.5, ALU.mult, ALU.add).then_inc(self.step, 1)
        dve.wait_ge(self.step, 4)
        dve.tensor_tensor(M.rs[:, :], M.rs[:, :], M.nt[:, :], ALU.mult).then_inc(self.step, 1)
        dve.wait_ge(self.step, 5)


def layernorm_stats(dve, M, s_stats, root):
    for b in range(NB):
        dve.bn_stats(M.stats[:, b, :], M.acc[:, b, :]).then_inc(s_stats, 1)
    for b in range(NB):
        dve.wait_ge(s_stats, b + 1)
        dve.bn_aggr(M.mv[:, b, :], M.stats[:, b, :]).then_inc(s_stats, 1)
    dve.wait_ge(s_stats, 2 * NB)
    dve.tensor_scalar(M.ve[:, :], M.mv[:, :, 1], EPS, None, ALU.add).then_inc(root.asked, 1)


def nf4_prepare(dve, chain, done, raw, norm, absmax, recip, width):
    blocks = width // QB
    cut = lambda t: t[:, 0:width].rearrange("p (n q) -> p n q", q=QB)
    dve.tensor_reduce(absmax[:, 0:blocks], cut(raw), AX.X, ALU.max, apply_absolute_value=True).then_inc(chain, 1)
    dve.wait_ge(chain, done(0))
    dve.scalar_tensor_tensor(recip[:, 0:blocks], absmax[:, 0:blocks], 0.0, absmax[:, 0:blocks],
                             op0=ALU.is_equal, op1=ALU.add).then_inc(chain, 1)
    dve.wait_ge(chain, done(1))
    dve.reciprocal(recip[:, 0:blocks], recip[:, 0:blocks]).then_inc(chain, 1)
    dve.wait_ge(chain, done(2))
    dve.tensor_tensor(cut(norm), cut(raw), recip[:, 0:blocks].unsqueeze(2).broadcast_to([P, blocks, QB]),
                      ALU.mult).then_inc(chain, 1)


def nf4_threshold(k):
    b = NF4_BOUNDS[k]
    return float(np.nextafter(b, np.float32(2.0))) if NF4_CODE[k + 1] <= 0 else float(b)


def nf4_level(dve, k, sign, code):
    if k == 0:
        return dve.tensor_scalar(code, sign, float(NF4_CODE[1]), float(NF4_CODE[0]), ALU.min, ALU.max)
    return dve.scalar_tensor_tensor(code, sign, float(NF4_CODE[k + 1]), code, op0=ALU.min, op1=ALU.max)


def nf4_finish(dve, raw, code, absmax, width):
    blocks = width // QB
    cut = lambda t: t[:, 0:width].rearrange("p (n q) -> p n q", q=QB)
    return dve.tensor_tensor(cut(raw), cut(code), absmax[:, 0:blocks].unsqueeze(2).broadcast_to([P, blocks, QB]),
                             ALU.mult)


def setup_phase(nc, M, sb, sem, x, ctx_in, mask, gains, lnw, nf4_src, wkv1):
    s_x = [sem(f"s_in_x{b}") for b in range(NB)]
    s_c = [sem(f"s_in_ctx{b}") for b in range(NB)]
    s_m, s_g, s_l, s_nf, s_w = (sem(f"s_in_{n}") for n in ("mask", "gains", "lnw", "nf4", "wkv1"))
    s_id = sem("s_ident")
    s_tg = sem("s_tanh")
    s_maskf = sem("s_maskf")
    s_stats = sem("s_ln0_stats")
    s_ms = sem("s_mean_square")
    s_x1 = sem("s_x1")
    s_acc = sem("s_acc_start")
    s_xn = sem("s_xn")
    s_wsplit = sem("s_wkv1_split")
    s_tr = sem("s_setup_transposed")
    s_hi = sem("s_setup_hi")
    s_lo = sem("s_setup_lo")
    s_kv = sem("s_kv1")
    s_k1 = sem("s_k1_hi")
    s_k1lo = sem("s_k1_lo")
    s_v1T = sem("s_v1T")
    s_v1 = sem("s_v1")
    s_kout = sem("s_k1_out")
    s_nchain, s_nsign, s_nlev, s_nout = (sem(f"s_tail_{n}") for n in ("chain", "sign", "level", "out"))
    ln_root = RootSteps(M, sem, "ln0")
    rms_root = RootSteps(M, sem, "rms")
    half = lambda j: slice(j * HALF, (j + 1) * HALF)

    with ExitStack() as local:
        c_nat = sb("c_nat", [P, NB, D], F32, local)
        x1 = sb("x1", [P, NB, D], F32, local)
        square = sb("square", [P, D], F32, local)
        mean_sq = sb("mean_sq", [P, NB], F32, local)
        lnw_b = sb("lnw_b", [P, D], F32, local)
        mask_words = sb("mask_words", [P, TOK // 4], I32, local)
        mask_u8 = mask_words.bitcast(U8)
        g_sb = sb("g_sb", [P, 4], F32, local)
        wkv = sb("wkv", [P, 2, KT * P], F32, local)
        wkv_hi = sb("wkv_hi", [P, 2, KT * P], F32R, local)
        wkv_lo = sb("wkv_lo", [P, 2, KT * P], F32R, local)
        k1_hi = sb("k1_hi", [P, TOK], F32R, local)
        k1_lo = sb("k1_lo", [P, TOK], F32R, local)
        v1T = sb("v1T", [P, TOK], F32, local)
        nraw = sb("ntail_raw", [P, NFTAIL], F32, local)
        nnorm = sb("ntail_norm", [P, NFTAIL], F32, local)
        ncode = sb("ntail_code", [P, NFTAIL], F32, local)
        nsign = sb("ntail_sign", [P, 2, NFTAIL], BF16, local)
        nabs = sb("ntail_abs", [P, NFTAIL // QB], F32, local)
        nrec = sb("ntail_rec", [P, NFTAIL // QB], F32, local)
        block = local.enter_context(nc.Block())
        tail = slice(H0 * NFC, NFW)
        by_k = lambda bank: bank[:, :].rearrange("p (k s) -> p k s", k=KT)

        @block.sync
        def _(sp):
            for b in range(NB):
                sp.dma_start(c_nat[:, b, :], ctx_in[b]).then_inc(s_c[b], 16)
            sp.dma_start(wkv[:, :, :], wkv1).then_inc(s_w, 16)
            for b in range(NB):
                sp.dma_start(M.acc[:, b, :], x[b]).then_inc(s_x[b], 16)
            sp.wait_ge(s_k1lo, 2)
            for part, src in enumerate((k1_hi, k1_lo)):
                for twice in range(2):
                    for h in range(KV1):
                        sp.dma_start(M.k1_dram[part, h, twice, :, :],
                                     src[h * DH1:(h + 1) * DH1, :].bitcast(F32)).then_inc(s_kout, 16)
            sp.wait_ge(s_nlev, NLEV + 1)
            sp.dma_start(M.nf4_dq[:, tail], nraw[:, :]).then_inc(s_nout, 16)
            sp.wait_ge(s_nout, 16)
            sp.wait_ge(s_kout, 16 * 4 * KV1)

        @block.gpsimd
        def _(pool):
            pool.memset(M.ident[:, :], 0.0).then_inc(s_id, 1)
            pool.memset(M.ident_b[:, :], 0.0).then_inc(s_id, 1)
            pool.wait_ge(s_id, 2)
            for t in (M.ident, M.ident_b):
                pool.affine_select(out=t[:, :], in_=t[:, :], compare_op=ALU.not_equal, fill=1.0, base=0,
                                   pattern=[[-1, P]], channel_multiplier=1).then_inc(s_id, 1)
            pool.memset(M.v1[:, :, :, :], 1.0).then_inc(s_id, 1)
            pool.wait_ge(s_w, 16)
            for m in range(2):
                pool.tensor_copy(wkv_hi[:, m, :], wkv[:, m, :]).then_inc(s_id, 1)

        @block.scalar
        def _(act):
            act.dma_start(g_sb[:, :], gains.partition_broadcast(P)).then_inc(s_g, 16)
            act.dma_start(nraw[:, :], nf4_src[:, tail]).then_inc(s_nf, 16)
            act.dma_start(mask_words[:, :].rearrange("p (b k) -> p b k", b=NB), mask.rearrange("b q k -> q b k")).then_inc(s_m, 16)
            act.dma_start(lnw_b[:, :], lnw.partition_broadcast(P)).then_inc(s_l, 16)
            act.wait_ge(s_g, 16)
            act.activation(M.tg[:, :], g_sb[:, :], ACT.Tanh).then_inc(s_tg, 1)
            for b in range(NB):
                act.wait_ge(s_tr, b + 1)
                act.activation(M.cT_hi[:, :, b * S:(b + 1) * S], by_k(M.pj[b % 4]), ACT.Copy).then_inc(s_hi, 1)
            for j in range(2):
                act.wait_ge(s_kv, j + 1)
                act.activation(k1_hi[:, half(j)], M.sc[j][:, :], ACT.Copy).then_inc(s_k1, 1)
            for j in range(2):
                act.wait_ge(s_kv, j + 3)
                act.activation(v1T[:, half(j)], M.tp[j][:, :], ACT.Copy).then_inc(s_v1T, 1)
            ln_root.scalar(act)
            for b in range(NB):
                act.wait_ge(s_x1, b + 1)
                if b:
                    act.wait_ge(s_ms, b)
                act.activation(square[:, :], x1[:, b, :], ACT.Square,
                               accum_out=mean_sq[:, b:b + 1]).then_inc(s_ms, 1)
            rms_root.scalar(act)
            act.wait_ge(s_nchain, 4)
            for k in range(NLEV):
                if k >= 2:
                    act.wait_ge(s_nlev, k - 1)
                act.activation(nsign[:, k % 2, :], nnorm[:, :], ACT.Sign, bias=-nf4_threshold(k)).then_inc(s_nsign, 1)
                if k >= NLEV - NB:
                    b = k - (NLEV - NB)
                    act.wait_ge(s_tr, NB + b + 1)
                    act.activation(M.xT_hi[:, :, b * S:(b + 1) * S], by_k(M.pj[b % 4]), ACT.Copy).then_inc(s_hi, 1)

        @block.vector
        def _(dve):
            def low(t):
                hi, lo, b = ((M.cT_hi, M.cT_lo, t) if t < NB else (M.xT_hi, M.xT_lo, t - NB))
                at = slice(b * S, (b + 1) * S)
                dve.wait_ge(s_hi, t + 1)
                dve.tensor_tensor(lo[:, :, at], by_k(M.pj[t % 4]), hi[:, :, at], ALU.subtract).then_inc(s_lo, 1)

            for b in range(NB):
                low(b)
            for m in range(2):
                dve.wait_ge(s_id, 6 + m)
                dve.tensor_tensor(wkv_lo[:, m, :], wkv[:, m, :], wkv_hi[:, m, :], ALU.subtract).then_inc(s_wsplit, 1)
            for b in range(NB):
                dve.wait_ge(s_x[b], 16)
                dve.bn_stats(M.stats[:, b, :], M.acc[:, b, :]).then_inc(s_stats, 1)
            for b in range(NB):
                dve.wait_ge(s_stats, b + 1)
                dve.bn_aggr(M.mv[:, b, :], M.stats[:, b, :]).then_inc(s_stats, 1)
            dve.wait_ge(s_stats, 2 * NB)
            dve.tensor_scalar(M.ve[:, :], M.mv[:, :, 1], EPS, None, ALU.add).then_inc(ln_root.asked, 1)
            dve.wait_ge(s_nf, 16)
            nf4_prepare(dve, s_nchain, lambda n: n + 1, nraw, nnorm, nabs, nrec, NFTAIL)
            for j in range(2):
                dve.wait_ge(s_k1, j + 1)
                dve.tensor_tensor(k1_lo[:, half(j)], M.sc[j][:, :], k1_hi[:, half(j)], ALU.subtract).then_inc(s_k1lo, 1)
            ln_root.vector(dve)
            for b in range(NB):
                dve.tensor_scalar(x1[:, b, :], M.acc[:, b, :], M.mv[:, b, 0:1], M.rs[:, b:b + 1],
                                  ALU.subtract, ALU.mult).then_inc(s_x1, 1)
            for j in range(2):
                dve.wait_ge(s_kv, j + 5)
                dve.wait_ge(s_id, 5)
                dve.tensor_copy(M.v1[:, QUAD * j:QUAD * (j + 1), :, 0:DH1].rearrange("p b n d -> p (b n) d"),
                                M.sc[j][:, :].rearrange("p (b d) -> p b d", d=DH1)).then_inc(s_v1, 1)
            dve.wait_ge(s_tg, 1)
            for b in range(NB):
                dve.wait_ge(s_x1, b + 1)
                dve.scalar_tensor_tensor(M.acc[:, b, :], x1[:, b, :], M.tg[:, 0:1], M.acc[:, b, :],
                                         op0=ALU.mult, op1=ALU.add).then_inc(s_acc, 1)
            dve.wait_ge(s_ms, NB)
            dve.tensor_scalar(M.ve[:, :], mean_sq[:, :], 1.0 / D, EPS, ALU.mult, ALU.add).then_inc(rms_root.asked, 1)
            rms_root.vector(dve)
            dve.wait_ge(s_l, 16)
            for b in range(NB):
                dve.scalar_tensor_tensor(x1[:, b, :], x1[:, b, :], M.rs[:, b:b + 1], lnw_b[:, :],
                                         op0=ALU.mult, op1=ALU.mult).then_inc(s_xn, 1)
            dve.wait_ge(s_m, 16)
            dve.tensor_scalar(M.maskneg[:, :], mask_u8[:, :], -1.0, -MASKED, ALU.add, ALU.mult).then_inc(s_maskf, 1)
            dve.tensor_reduce(M.rowany[:, :], mask_u8[:, :].rearrange("p (b k) -> p b k", b=NB), AX.X,
                              ALU.max).then_inc(s_maskf, 1)
            for k in range(NLEV):
                dve.wait_ge(s_nsign, k + 1)
                if k:
                    dve.wait_ge(s_nlev, k)
                nf4_level(dve, k, nsign[:, k % 2, :], ncode[:, :]).then_inc(s_nlev, 1)
                if k >= NLEV - NB:
                    low(NB + k - (NLEV - NB))
            dve.wait_ge(s_nlev, NLEV)
            nf4_finish(dve, nraw, ncode, nabs, NFTAIL).then_inc(s_nlev, 1)

        @block.tensor
        def _(pe):
            def transposed(t):
                src, b = ((c_nat, t) if t < NB else (x1, t - NB))
                if t < NB:
                    pe.wait_ge(s_c[b], 16)
                else:
                    pe.wait_ge(s_xn, b + 1)
                if t >= 4:
                    pe.wait_ge(s_lo, t - 3)
                for k in range(KT):
                    mm = pe.transpose(M.pj[t % 4][:, k * P:(k + 1) * P], src[:, b, k * P:(k + 1) * P], M.ident[:, :])
                mm.then_inc(s_tr, 1)

            pe.wait_ge(s_id, 4)
            for t in range(NB):
                transposed(t)
            pe.wait_ge(s_lo, NB)
            for m, banks in enumerate((M.sc, M.tp)):
                pe.wait_ge(s_wsplit, m + 1)
                for j in range(2):
                    for k in range(KT):
                        w = slice(k * P, (k + 1) * P)
                        pe.matmul(banks[j][:, :], wkv_hi[:, m, w], M.cT_hi[:, k, half(j)], start=(k == 0), stop=False)
                        pe.matmul(banks[j][:, :], wkv_hi[:, m, w], M.cT_lo[:, k, half(j)], start=False, stop=False)
                        mm = pe.matmul(banks[j][:, :], wkv_lo[:, m, w], M.cT_hi[:, k, half(j)], start=False,
                                       stop=(k == KT - 1))
                    mm.then_inc(s_kv, 1)
            for j in range(2):
                pe.wait_ge(s_v1T, j + 1)
                pe.wait_ge(s_k1lo, j + 1)
                for b in range(QUAD):
                    mm = pe.transpose(M.sc[j][:, b * S:(b + 1) * S],
                                      v1T[:, (QUAD * j + b) * S:(QUAD * j + b + 1) * S], M.ident[:, :])
                mm.then_inc(s_kv, 1)
            for t in range(NB, 2 * NB):
                transposed(t)


PJ_USES = ([("v", 0, b) for b in range(NB)]
           + [(m, h, half) for h in (1, 2, 3) for m in "qk" for half in (0, 1)]
           + [("o", 0, t) for t in range(NB)]
           + [(m, GH, half) for m in "qk" for half in (0, 1)]
           + [("o", 1, t) for t in range(NB)])
N_PJ = len(PJ_USES)
N_O = 2 * NB
N_EV = N_PJ - N_O
PRIOR_PJ = PJ_USES.index(("q", GH, 0))
SPLITS = [("q", 1), ("k", 1), ("o", 0), ("o", 1), ("q", 2), ("v", 0), ("k", 2), ("v", 1), ("q", 3), ("v", 2), ("k", 3),
          ("v", 3), ("q", GH), ("k", GH), ("o", 2), ("o", 3)]
N_SP = len(SPLITS)
N_NF = GH * NLEV


def attention0_phase(nc, M, sb, sem, pbias, wqk0, wv0, wo0, nf4_src):
    s_raw_qk = [sem(f"s_raw_qk{i}") for i in range(2)]
    s_raw_v = [sem(f"s_raw_v{i}") for i in range(2)]
    s_raw_o = [sem(f"s_raw_o{i}") for i in range(2)]
    s_bias = sem("s_bias")
    s_whi = sem("s_whi")
    s_wlo = sem("s_wlo")
    s_pj = sem("s_pj")
    s_ev = sem("s_ev")
    s_oadd = sem("s_oadd")
    s_score = sem("s_score")
    s_biased = sem("s_biased")
    s_max = sem("s_max")
    s_exp = sem("s_exp")
    s_rsum = sem("s_rsum")
    s_prob = sem("s_prob")
    s_pT = sem("s_pT")
    s_pTc = sem("s_pTc")
    s_pv = sem("s_pv")
    s_ahi = sem("s_ahi")
    s_alo = sem("s_alo")
    s_nin = [sem(f"s_nin{i}") for i in range(GH)]
    s_nout = [sem(f"s_nout0_{i}") for i in range(GH)]
    s_nprep = sem("s_nprep")
    s_nsign = sem("s_nsign")
    s_nlev = sem("s_nlev")
    s_turn = sem("s_turn")
    s_ndq = sem("s_ndq")

    pj_at = {u: n for n, u in enumerate(PJ_USES)}
    o_at = {u: n for n, u in enumerate([u for u in PJ_USES if u[0] == "o"])}
    ev_at = {u: n for n, u in enumerate([u for u in PJ_USES if u[0] != "o"])}
    split_at = {u: n for n, u in enumerate(SPLITS)}
    half = lambda j: slice(j * HALF, (j + 1) * HALF)
    tile = lambda b: slice(b * S, (b + 1) * S)
    in_half = lambda b: slice((b % QUAD) * S, (b % QUAD + 1) * S)

    with ExitStack() as local:
        raw_qk = sb("raw_qk", [P, 2, 2, KT * DH0], F32, local)
        qk_hi = sb("qk_hi", [P, 2, KT * DH0], F32R, local)
        qk_lo = sb("qk_lo", [P, 2, KT * DH0], F32R, local)
        raw_v = sb("raw_v", [P, 2, GH * DH0], F32, local)
        v_hi = sb("v_hi", [P, KT, GH * DH0], F32R, local)
        v_lo = sb("v_lo", [P, KT, GH * DH0], F32R, local)
        raw_o = sb("raw_o", [P, 2, D], F32, local)
        o_hi = sb("o_hi", [P, 2, D], F32R, local)
        o_lo = sb("o_lo", [P, 2, D], F32R, local)
        bias_sb = sb("bias_sb", [P, GH, S], F32, local)
        qT = sb("qT", [P, TOK], F32, local)
        kT = sb("kT", [P, TOK], F32, local)
        V = sb("V", [P, NB, GH * DH0], F32, local)
        prob = sb("prob", [P, 2, TOK], F32, local)
        probT = sb("probT", [P, TOK], F32, local)
        a_hi = sb("a_hi", [P, 3, TOK], F32R, local)
        a_lo = sb("a_lo", [P, 3, TOK], F32R, local)
        nmax = sb("nmax", [P, 2, NB], F32, local)
        rsum = sb("rsum", [P, 2, NB], F32, local)
        nraw = sb("nraw", [P, GH, NFC], F32, local)
        nnorm = sb("nnorm", [P, 2, NFC], F32, local)
        ncode = sb("ncode", [P, NFC], F32, local)
        nsign = sb("nsign", [P, 4, NFC], BF16, local)
        nabs = sb("nabs", [P, 2, NFC // QB], F32, local)
        nrec = sb("nrec", [P, NFC // QB], F32, local)
        slot = lambda h: h % 3
        block = local.enter_context(nc.Block())

        @block.sync
        def _(sp):
            def load_qk(g, h):
                sp.wait_ge(s_wlo, nth(N_SP, g, split_at["k", h - 2] if h > 2 else split_at["k", h + 2] - N_SP))
                sp.dma_start(raw_qk[:, h % 2, :, :].rearrange("p m n -> p (m n)"), wqk0[g * GH + h]).then_inc(s_raw_qk[h % 2], 16)

            def load_o(g, h):
                sp.wait_ge(s_wlo, nth(N_SP, g, split_at["o", h - 2] if h >= 2 else split_at["o", h + 2] - N_SP))
                sp.dma_start(raw_o[:, h % 2, :], wo0[g * GH + h]).then_inc(s_raw_o[h % 2], 16)

            def load_v(g, i):
                sp.wait_ge(s_wlo, nth(N_SP, g, split_at["v", i - 2] if i >= 2 else split_at["v", i + 2] - N_SP))
                sp.dma_start(raw_v[:, i % 2, :], wv0[g + 1, i]).then_inc(s_raw_v[i % 2], 16)

            sp.dma_start(raw_qk[:, 0, :, :].rearrange("p m n -> p (m n)"), wqk0[0]).then_inc(s_raw_qk[0], 16)
            for i in range(KT):
                if i >= 2:
                    sp.wait_ge(s_wlo, nth(N_SP, -1, split_at["v", i - 2]))
                sp.dma_start(raw_v[:, i % 2, :], wv0[0, i]).then_inc(s_raw_v[i % 2], 16)
            with sp.Fori(0, GROUPS) as g:
                load_qk(g, 1)
                load_o(g, 0)
                load_o(g, 1)
                sp.wait_ge(s_biased, nth(2 * GH, g, -1))
                sp.dma_start(bias_sb[:, :, :], pbias[g]).then_inc(s_bias, 16)
                load_qk(g, 2)
                load_v(g, 0)
                load_v(g, 1)
                load_qk(g, 3)
                load_o(g, 2)
                load_o(g, 3)
                load_qk(g, GH)
                load_v(g, 2)
                load_v(g, 3)

        @block.gpsimd
        def _(pool):
            def split(g, m, i):
                if m == "v":
                    dst, low, src, arrived = v_hi[:, i, :], v_lo[:, i, :], raw_v[:, i % 2, :], s_raw_v[i % 2]
                    reader, count = pj_at["v", 0, NB - 1], (g + 1) * 32 + 16 * (i // 2 + 1)
                elif m == "o":
                    dst, low, src, arrived = o_hi[:, i % 2, :], o_lo[:, i % 2, :], raw_o[:, i % 2, :], s_raw_o[i % 2]
                    reader, count = (pj_at["o", 0, NB - 1] if i >= 2 else -1), g * 32 + 16 * (i // 2 + 1)
                else:
                    mi = "qk".index(m)
                    dst, low, src, arrived = qk_hi[:, mi, :], qk_lo[:, mi, :], raw_qk[:, i % 2, mi, :], s_raw_qk[i % 2]
                    reader, count = (pj_at[m, i - 1, 1] if i > 1 else pj_at[m, GH, 1] - N_PJ), g * 32 + 16 * (i // 2 + 1)
                pool.wait_ge(s_pj, nth(N_PJ, g, reader))
                pool.wait_ge(arrived, count)
                pool.sem_inc(s_turn, 1)
                pool.tensor_copy(dst, src).then_inc(s_whi, 1)
                pool.wait_ge(s_whi, nth(N_SP, g, split_at[m, i]))
                pool.sem_inc(s_turn, 1)
                pool.tensor_tensor(low, src, dst, ALU.subtract).then_inc(s_wlo, 1)

            def load_nf4(g, c):
                pool.wait_ge(s_nout[c], nth(16, g, -1))
                pool.dma_start(nraw[:, c, :], nf4_src[:, bass.ts(g * GH + c, NFC)]).then_inc(s_nin[c], 16)

            for n, (m, i) in enumerate(SPLITS):
                if m == "v" or i == GH:
                    split(-1, m, i)
                    pool.wait_ge(s_wlo, n + 1)
                else:
                    pool.sem_inc(s_whi, 1)
                    pool.sem_inc(s_wlo, 1)
            with pool.Fori(0, GROUPS) as g:
                for n, (m, i) in enumerate(SPLITS):
                    if n < GH:
                        load_nf4(g, n)
                    split(g, m, i)

        @block.scalar
        def _(act):
            act.sem_inc(s_ev, N_EV - 4)
            act.sem_inc(s_nsign, N_NF)
            for s in (s_exp, s_pTc, s_ahi):
                act.sem_inc(s, 2 * GH)
            for c in range(GH):
                act.sem_inc(s_nout[c], 16)

            def evacuate(m, h, j, g):
                n = pj_at[m, h, j]
                act.wait_ge(s_pj, nth(N_PJ, g, n))
                dst = V[:, j, :] if m == "v" else (qT if m == "q" else kT)[:, half(j)]
                act.activation(dst, M.pj[n % 4][:, :], ACT.Copy).then_inc(s_ev, 1)

            for m in "qk":
                for j in range(2):
                    evacuate(m, GH, j, -1)
            with act.Fori(0, GROUPS) as g:
                level = [0]

                def nf4_out(c):
                    act.wait_ge(s_ndq, nth(GH, g, c))
                    act.dma_start(M.nf4_dq[:, bass.ts(g * GH + c, NFC)], nraw[:, c, :]).then_inc(s_nout[c], 16)

                def nf4_signs(n):
                    for k in range(level[0], level[0] + n):
                        c, lev = divmod(k, NLEV)
                        if lev == 5 and c:
                            nf4_out(c - 1)
                        if lev == 0:
                            act.wait_ge(s_nprep, nth(4 * GH, g, 4 * c + 3))
                        act.wait_ge(s_nlev, nth(N_NF, g, k - 4))
                        act.activation(nsign[:, k % 4, :], nnorm[:, c % 2, :], ACT.Sign,
                                       bias=-nf4_threshold(lev)).then_inc(s_nsign, 1)
                    level[0] += n

                def exps(h):
                    for j in range(2):
                        act.wait_ge(s_max, nth(2 * GH, g, 2 * h + j))
                        for b in range(QUAD * j, QUAD * (j + 1)):
                            e = act.activation(prob[:, h % 2, tile(b)], prob[:, h % 2, tile(b)], ACT.Exp,
                                               bias=nmax[:, h % 2, b:b + 1], accum_out=rsum[:, h % 2, b:b + 1])
                        e.then_inc(s_exp, 1)

                def copy_probT(h):
                    for j in range(2):
                        act.wait_ge(s_pT, nth(2 * GH, g, 2 * h + j))
                        act.activation(probT[:, half(j)], M.tp[j][:, :], ACT.Copy).then_inc(s_pTc, 1)

                def attn_high(h):
                    for j in range(2):
                        act.wait_ge(s_pv, nth(2 * GH, g, 2 * h + j))
                        act.activation(a_hi[:, slot(h), half(j)], M.tp[j][:, :], ACT.Copy).then_inc(s_ahi, 1)

                evacuate("v", 0, 0, g)
                exps(0)
                evacuate("v", 0, 1, g)
                nf4_signs(2)
                for b in range(2, NB):
                    evacuate("v", 0, b, g)
                    nf4_signs(3 if b < 4 else 2)
                for h in (1, 2, 3):
                    if h > 1:
                        exps(h - 1)
                    evacuate("q", h, 0, g)
                    evacuate("q", h, 1, g)
                    nf4_signs(2 if h == 1 else 1)
                    evacuate("k", h, 0, g)
                    copy_probT(h - 1)
                    nf4_signs(2)
                    evacuate("k", h, 1, g)
                    attn_high(h - 1)
                    nf4_signs(4)
                exps(3)
                nf4_signs(1)
                evacuate("q", GH, 0, g)
                nf4_signs(2)
                evacuate("q", GH, 1, g)
                nf4_signs(1)
                evacuate("k", GH, 0, g)
                copy_probT(3)
                nf4_signs(1)
                evacuate("k", GH, 1, g)
                attn_high(3)
                nf4_signs(N_NF - level[0])
                nf4_out(GH - 1)
            for c in range(GH):
                act.wait_ge(s_nout[c], 16 * (GROUPS + 1))

        @block.vector
        def _(dve):
            for s, n in ((s_oadd, N_O), (s_biased, 2 * GH), (s_max, 2 * GH), (s_prob, 2 * GH),
                         (s_alo, 2 * GH), (s_nprep, 4 * GH), (s_nlev, N_NF), (s_ndq, GH), (s_rsum, 4 * GH)):
                dve.sem_inc(s, n)

            with dve.Fori(0, GROUPS) as g:
                level = [0]

                def nf4_begin(c):
                    dve.wait_ge(s_nin[c], g * 16 + 16)
                    nf4_prepare(dve, s_nprep, lambda n: nth(4 * GH, g, 4 * c + n), nraw[:, c, :], nnorm[:, c % 2, :],
                                nabs[:, c % 2, :], nrec, NFC)

                def nf4_levels(n):
                    for k in range(level[0], level[0] + n):
                        c, lev = divmod(k, NLEV)
                        dve.wait_ge(s_nsign, nth(N_NF, g, k))
                        dve.wait_ge(s_nlev, nth(N_NF, g, k - 1))
                        if lev == 0:
                            dve.wait_ge(s_ndq, nth(GH, g, c - 1))
                        nf4_level(dve, lev, nsign[:, k % 4, :], ncode[:, :]).then_inc(s_nlev, 1)
                        if lev == NLEV // 2 and c < GH - 1:
                            nf4_begin(c + 1)
                        if lev == NLEV - 1:
                            dve.wait_ge(s_nlev, nth(N_NF, g, k))
                            nf4_finish(dve, nraw[:, c, :], ncode, nabs[:, c % 2, :], NFC).then_inc(s_ndq, 1)
                    level[0] += n

                def bias_and_max(h):
                    for j in range(2):
                        part = prob[:, h % 2, half(j)].rearrange("p (b k) -> p b k", b=QUAD)
                        dve.wait_ge(s_score, nth(2 * GH, g, 2 * h + j))
                        dve.tensor_tensor(part, M.sc[j][:, :].rearrange("p (b k) -> p b k", b=QUAD),
                                          bias_sb[:, h:h + 1, :].broadcast_to([P, QUAD, S]), ALU.add).then_inc(s_biased, 1)
                        dve.wait_ge(s_biased, nth(2 * GH, g, 2 * h + j))
                        dve.tensor_reduce(nmax[:, h % 2, QUAD * j:QUAD * (j + 1)], part, AX.X, ALU.max,
                                          negate=True).then_inc(s_max, 1)

                def normalize(h):
                    for j in range(2):
                        sums = rsum[:, h % 2, QUAD * j:QUAD * (j + 1)]
                        dve.wait_ge(s_exp, nth(2 * GH, g, 2 * h + j))
                        dve.reciprocal(sums, sums).then_inc(s_rsum, 1)
                        dve.wait_ge(s_rsum, nth(4 * GH, g, 4 * h + 2 * j))
                        dve.tensor_tensor(sums, sums, M.rowany[:, QUAD * j:QUAD * (j + 1)], ALU.mult).then_inc(s_rsum, 1)
                        dve.wait_ge(s_rsum, nth(4 * GH, g, 4 * h + 2 * j + 1))
                        for b in range(QUAD * j, QUAD * (j + 1)):
                            last = dve.tensor_scalar(prob[:, h % 2, tile(b)], prob[:, h % 2, tile(b)],
                                                     rsum[:, h % 2, b:b + 1], None, ALU.mult)
                        last.then_inc(s_prob, 1)

                def attn_low(h):
                    for j in range(2):
                        dve.wait_ge(s_ahi, nth(2 * GH, g, 2 * h + j))
                        dve.tensor_tensor(a_lo[:, slot(h), half(j)], M.tp[j][:, :], a_hi[:, slot(h), half(j)],
                                          ALU.subtract).then_inc(s_alo, 1)

                def add_out(pair, t):
                    n = pj_at["o", pair, t]
                    dve.wait_ge(s_pj, nth(N_PJ, g, n))
                    dve.wait_ge(s_oadd, nth(N_O, g, o_at["o", pair, t] - NB))
                    dve.scalar_tensor_tensor(M.acc[:, t, :], M.pj[n % 4][:, :], M.tg[:, 0:1], M.acc[:, t, :],
                                             op0=ALU.mult, op1=ALU.add).then_inc(s_oadd, 1)

                dve.wait_ge(s_bias, g * 16 + 16)
                bias_and_max(0)
                nf4_begin(0)
                nf4_levels(2)
                normalize(0)
                nf4_levels(12)
                for h in (1, 2, 3):
                    if h > 1:
                        bias_and_max(h - 1)
                        normalize(h - 1)
                    nf4_levels(6 if h == 1 else 5)
                    attn_low(h - 1)
                    nf4_levels(2)
                bias_and_max(3)
                for t in range(4):
                    add_out(0, t)
                normalize(3)
                for t in range(4, NB):
                    add_out(0, t)
                    nf4_levels(1 if t < NB - 1 else 4)
                attn_low(3)
                for t in range(NB):
                    add_out(1, t)
                    nf4_levels(2 if t < NB - 1 else N_NF - level[0])

        @block.tensor
        def _(pe):
            pe.sem_inc(s_pj, PRIOR_PJ)
            pe.sem_inc(s_score, 2 * GH)
            pe.sem_inc(s_pT, 2 * GH)
            pe.sem_inc(s_pv, 2 * GH)
            def take(m, h, j, g):
                n = pj_at[m, h, j]
                was = PJ_USES[n - 4]
                if was[0] == "o":
                    pe.wait_ge(s_oadd, nth(N_O, g, o_at[was] - (0 if n >= 4 else N_O)))
                else:
                    pe.wait_ge(s_ev, nth(N_EV, g, ev_at[was]))
                return M.pj[n % 4]

            def three_pass(bank, w, wl, m, ml, first, last):
                pe.matmul(bank, w, m, start=first, stop=False)
                pe.matmul(bank, w, ml, start=False, stop=False)
                return pe.matmul(bank, wl, m, start=False, stop=last)

            def project(m, h, j, g):
                bank = take(m, h, j, g)
                if j == 0:
                    pe.wait_ge(s_wlo, nth(N_SP, g, split_at[m, h]))
                mi = "qk".index(m)
                hi, lo = (M.xT_hi, M.xT_lo) if m == "q" else (M.cT_hi, M.cT_lo)
                for k in range(KT):
                    w = slice(k * DH0, (k + 1) * DH0)
                    mm = three_pass(bank[:, :], qk_hi[:, mi, w], qk_lo[:, mi, w], hi[:, k, half(j)],
                                    lo[:, k, half(j)], k == 0, k == KT - 1)
                mm.then_inc(s_pj, 1)

            for m in "qk":
                for j in range(2):
                    project(m, GH, j, -1)
            pe.wait_ge(s_pj, PRIOR_PJ + 4)
            pe.sem_inc(s_pj, N_PJ - PRIOR_PJ - 4)
            with pe.Fori(0, GROUPS) as g:
                def values(b):
                    bank = take("v", 0, b, g)
                    for k in range(KT):
                        if b == 0:
                            pe.wait_ge(s_wlo, nth(N_SP, g, split_at["v", k] - N_SP))
                        mm = three_pass(bank[:, :], M.cT_hi[:, k, tile(b)], M.cT_lo[:, k, tile(b)], v_hi[:, k, :],
                                        v_lo[:, k, :], k == 0, k == KT - 1)
                    mm.then_inc(s_pj, 1)

                def scores(h):
                    pe.wait_ge(s_ev, nth(N_EV, g, ev_at["k", h, 1] if h else ev_at["k", GH, 1] - N_EV))
                    for j in range(2):
                        pe.wait_ge(s_biased, nth(2 * GH, g, 2 * h + j - 2))
                        pe.matmul(M.sc[j][:, :], M.ident_b[:, :], M.maskneg[:, half(j)], start=True, stop=False)
                        for b in range(QUAD * j, QUAD * (j + 1)):
                            mm = pe.matmul(M.sc[j][:, in_half(b)], qT[:, tile(b)], kT[:, tile(b)], start=False,
                                           stop=(b % QUAD == QUAD - 1))
                        mm.then_inc(s_score, 1)

                def transpose_probs(h):
                    for j in range(2):
                        pe.wait_ge(s_prob, nth(2 * GH, g, 2 * h + j))
                        pe.wait_ge(s_alo, nth(2 * GH, g, 2 * h + j - 2))
                        for b in range(QUAD * j, QUAD * (j + 1)):
                            mm = pe.transpose(M.tp[j][:, in_half(b)], prob[:, h % 2, tile(b)], M.ident[:, :])
                        mm.then_inc(s_pT, 1)

                def weigh_values(h):
                    for j in range(2):
                        pe.wait_ge(s_pTc, nth(2 * GH, g, 2 * h + j))
                        for b in range(QUAD * j, QUAD * (j + 1)):
                            mm = pe.matmul(M.tp[j][:, in_half(b)], V[:, b, h * DH0:(h + 1) * DH0], probT[:, tile(b)],
                                           start=True, stop=True)
                        mm.then_inc(s_pv, 1)

                def project_out(pair, t):
                    bank = take("o", pair, t, g)
                    if t == 0:
                        pe.wait_ge(s_wlo, nth(N_SP, g, split_at["o", 2 * pair + 1]))
                    pe.wait_ge(s_alo, nth(2 * GH, g, 2 * (2 * pair + 1) + t // QUAD))
                    for h in (2 * pair, 2 * pair + 1):
                        mm = three_pass(bank[:, :], a_hi[:, slot(h), tile(t)], a_lo[:, slot(h), tile(t)],
                                        o_hi[:, h % 2, :], o_lo[:, h % 2, :], h % 2 == 0, h % 2 == 1)
                    mm.then_inc(s_pj, 1)

                scores(0)
                for b in range(NB):
                    values(b)
                for h in (1, 2, 3):
                    project("q", h, 0, g)
                    project("q", h, 1, g)
                    project("k", h, 0, g)
                    transpose_probs(h - 1)
                    project("k", h, 1, g)
                    weigh_values(h - 1)
                    scores(h)
                for t in range(NB):
                    project_out(0, t)
                project("q", GH, 0, g)
                project("q", GH, 1, g)
                project("k", GH, 0, g)
                transpose_probs(3)
                project("k", GH, 1, g)
                weigh_values(3)
                for t in range(NB):
                    project_out(1, t)


def attention1_phase(nc, M, sb, sem, wq1, wo1):
    W = REP1 * S
    UNITS = 2 * NB
    s_wraw = sem("s_a1_wraw")
    s_w = sem("s_a1_w")
    s_proj = sem("s_a1_proj")
    s_qhi = sem("s_a1_qhi")
    s_qlo = sem("s_a1_qlo")
    s_zero = sem("s_a1_zero")
    s_in = [sem(f"s_a1_in{i}") for i in range(2)]
    s_score = sem("s_a1_score")
    s_nmax = sem("s_a1_nmax")
    s_sub = sem("s_a1_sub")
    s_exp = sem("s_a1_exp")
    s_pT = sem("s_a1_pT")
    s_pTc = sem("s_a1_pTc")
    s_pv = sem("s_a1_pv")
    s_rec = sem("s_a1_rec")
    s_att = sem("s_a1_att")
    s_aT, s_ahi, s_alo, s_out, s_acc = (sem(f"s_a1_{n}") for n in ("aT", "ahi", "alo", "out", "acc"))
    half = lambda j: slice(j * HALF, (j + 1) * HALF)
    tile = lambda b: slice(b * S, (b + 1) * S)

    with ExitStack() as local:
        w_raw = sb("w1_raw", [P, KT, D], F32, local)
        w_hi = sb("w1_hi", [P, KT, D], F32R, local)
        w_lo = sb("w1_lo", [P, KT, D], F32R, local)
        q_hi = sb("q1_hi", [P, KT, TOK], F32R, local)
        q_lo = sb("q1_lo", [P, KT, TOK], F32R, local)
        k_hi = sb("k1d_hi", [P, 2, NB, REP1, S], F32R, local)
        k_lo = sb("k1d_lo", [P, 2, NB, REP1, S], F32R, local)
        qr = sb("qr", [P, 2, TOK], F32R, local)
        prob = sb("prob1", [P, 4, W], F32, local)
        probT = sb("probT1", [P, 2, W], F32, local)
        nmax = sb("nmax1", [P, 4, REP1], F32, local)
        rec = sb("rec1", [P, 2, QUAD, REP1], F32, local)
        att = sb("att1", [P, NB, D], F32, local)
        ln = LayerNorm(M, sem, "a1_ln", att)
        av = [t[:, 0:QUAD * REP1 * (DH1 + 1)].rearrange("p (b a d) -> p b a d", b=QUAD, a=REP1) for t in M.sc]
        block = local.enter_context(nc.Block())
        DMAS = 4 * REP1

        @block.sync
        def _(sp):
            sp.dma_start(w_raw[:, :, :], wq1).then_inc(s_wraw, 16)
            sp.wait_ge(s_zero, 4)
            sp.wait_ge(s_qlo, 2 * KT)
            with sp.Fori(0, KV1 // 2) as g:
                for par in range(2):
                    sp.wait_ge(s_pv, nth(UNITS, g, par * NB + NB - 1 - UNITS))
                    for a in range(REP1):
                        rows = slice(32 * a, 32 * a + 32)
                        src = slice(64 * par + DH1 * a, 64 * par + DH1 * (a + 1))
                        for part, dst in enumerate((k_hi, k_lo)):
                            sp.dma_start(dst[rows, par, :, a, :].bitcast(F32),
                                         M.k1_dram[part, g * 2 + par].rearrange("c d (b k) -> (c d) b k", k=S)).then_inc(s_in[par], 16)
                        for part, s_src in enumerate((q_hi, q_lo)):
                            to = 32 * a + DH1 * part
                            sp.dma_start(qr[to:to + DH1, par, :].bitcast(F32), s_src[src, g, :].bitcast(F32)).then_inc(s_in[par], 16)
            sp.wait_ge(s_w, 2)
            sp.dma_start(w_raw[:, :, :], wo1).then_inc(s_wraw, 16)

        @block.gpsimd
        def _(pool):
            for t in (k_hi, k_lo):
                for par in range(2):
                    pool.memset(t[:, par, :, :, :].rearrange("p b a k -> p (b a k)").bitcast(F32), 0.0).then_inc(s_zero, 1)

        @block.scalar
        def _(act):
            act.sem_inc(s_exp, UNITS)
            act.sem_inc(s_pTc, UNITS)
            act.wait_ge(s_wraw, 16)
            act.activation(w_hi[:, :, :], w_raw[:, :, :], ACT.Copy).then_inc(s_w, 1)
            ln.scalar(act)
            for n in range(2 * KT):
                act.wait_ge(s_proj, n + 1)
                act.activation(q_hi[:, n // 2, half(n % 2)], M.pj[n % 4][:, :], ACT.Copy, scale=DH1 ** -0.5).then_inc(s_qhi, 1)
            with act.Fori(0, KV1 // 2) as g:
                for n in range(UNITS + 2):
                    if n < UNITS:
                        act.wait_ge(s_sub, nth(UNITS, g, n))
                        act.activation(prob[:, n % 4, :], prob[:, n % 4, :], ACT.Exp).then_inc(s_exp, 1)
                    if n >= 2:
                        m = n - 2
                        act.wait_ge(s_pT, nth(UNITS, g, m))
                        act.wait_ge(s_pv, nth(UNITS, g, m - 2))
                        act.activation(probT[:, m % 2, :], M.tp[m % 2][:, :], ACT.Copy).then_inc(s_pTc, 1)
            act.wait_ge(s_wraw, 32)
            act.activation(w_hi[:, :, :], w_raw[:, :, :], ACT.Copy).then_inc(s_w, 1)
            for b in range(NB):
                act.wait_ge(s_aT, b + 1)
                act.activation(M.xT_hi[:, :, tile(b)], M.pj[b % 2][:, :].rearrange("p (k s) -> p k s", k=KT),
                               ACT.Copy).then_inc(s_ahi, 1)

        @block.vector
        def _(dve):
            for s, n in ((s_nmax, UNITS), (s_sub, UNITS), (s_rec, 4), (s_att, 4)):
                dve.sem_inc(s, n)
            dve.wait_ge(s_w, 1)
            dve.tensor_tensor(w_lo[:, :, :], w_raw[:, :, :], w_hi[:, :, :], ALU.subtract).then_inc(s_w, 1)
            ln.vector(dve)
            for n in range(2 * KT):
                dve.wait_ge(s_qhi, n + 1)
                dve.scalar_tensor_tensor(q_lo[:, n // 2, half(n % 2)], M.pj[n % 4][:, :], DH1 ** -0.5,
                                         q_hi[:, n // 2, half(n % 2)], op0=ALU.mult, op1=ALU.subtract).then_inc(s_qlo, 1)
            with dve.Fori(0, KV1 // 2) as g:
                def finish_quad(q):
                    dve.wait_ge(s_pv, nth(UNITS, g, QUAD * q + QUAD - 1))
                    dve.reciprocal(rec[:, q % 2, :, :], av[q % 2][:, :, :, DH1]).then_inc(s_rec, 1)
                    dve.wait_ge(s_rec, nth(4, g, q))
                    b = QUAD * (q % 2)
                    for i in range(QUAD):
                        dst = att[:, b + i, bass.ds(g * (2 * REP1 * DH1) + (q // 2) * REP1 * DH1, REP1 * DH1)]
                        last = dve.tensor_tensor(dst.rearrange("p (a d) -> p a d", a=REP1), av[q % 2][:, i, :, 0:DH1],
                                                 rec[:, q % 2, i, :].unsqueeze(2).broadcast_to([P, REP1, DH1]), ALU.mult)
                    last.then_inc(s_att, 1)

                for n in range(UNITS + 4):
                    if n < UNITS:
                        dve.wait_ge(s_score, nth(UNITS, g, n))
                        scores = M.pj[n % 4][:, :].rearrange("p (a k) -> p a k", a=REP1)
                        dve.tensor_reduce(nmax[:, n % 4, :], scores, AX.X, ALU.max, negate=True).then_inc(s_nmax, 1)
                        dve.wait_ge(s_nmax, nth(UNITS, g, n))
                        dve.tensor_tensor(prob[:, n % 4, :].rearrange("p (a k) -> p a k", a=REP1), scores,
                                          nmax[:, n % 4, :].unsqueeze(2).broadcast_to([P, REP1, S]), ALU.add).then_inc(s_sub, 1)
                    if n >= 7 and (n - 7) % 4 == 0:
                        finish_quad((n - 7) // 4)
            dve.wait_ge(s_w, 3)
            dve.tensor_tensor(w_lo[:, :, :], w_raw[:, :, :], w_hi[:, :, :], ALU.subtract).then_inc(s_w, 1)

            def low(b):
                dve.wait_ge(s_ahi, b + 1)
                dve.tensor_tensor(M.xT_lo[:, :, tile(b)], M.pj[b % 2][:, :].rearrange("p (k s) -> p k s", k=KT),
                                  M.xT_hi[:, :, tile(b)], ALU.subtract).then_inc(s_alo, 1)

            low(0)
            for b in range(NB):
                if b + 1 < NB:
                    low(b + 1)
                dve.wait_ge(s_out, b + 1)
                dve.scalar_tensor_tensor(M.acc[:, b, :], M.pj[2 + b % 2][:, :], M.tg[:, 1:2], M.acc[:, b, :],
                                         op0=ALU.mult, op1=ALU.add).then_inc(s_acc, 1)

        @block.tensor
        def _(pe):
            pe.sem_inc(s_score, UNITS)
            pe.sem_inc(s_pT, UNITS)
            pe.sem_inc(s_pv, UNITS)
            ln.tensor(pe)
            pe.wait_ge(s_w, 2)
            for n in range(2 * KT):
                t, j = divmod(n, 2)
                if n >= 4:
                    pe.wait_ge(s_qlo, n - 3)
                for k in range(KT):
                    hi, lo = w_hi[:, k, t * P:(t + 1) * P], w_lo[:, k, t * P:(t + 1) * P]
                    bank = M.pj[n % 4][:, :]
                    pe.matmul(bank, hi, M.xT_hi[:, k, half(j)], start=(k == 0), stop=False)
                    pe.matmul(bank, hi, M.xT_lo[:, k, half(j)], start=False, stop=False)
                    mm = pe.matmul(bank, lo, M.xT_hi[:, k, half(j)], start=False, stop=(k == KT - 1))
                mm.then_inc(s_proj, 1)
            pe.wait_ge(s_qlo, 2 * KT)
            with pe.Fori(0, KV1 // 2) as g:
                for n in range(UNITS + 3):
                    if n < UNITS:
                        par, b = divmod(n, NB)
                        if b == 0:
                            pe.wait_ge(s_in[par], g * (16 * DMAS) + 16 * DMAS)
                        pe.wait_ge(s_sub, nth(UNITS, g, n - 4))
                        pe.matmul(M.pj[n % 4][:, :], qr[:, par, tile(b)], k_hi[:, par, b, :, :], start=True, stop=False)
                        pe.matmul(M.pj[n % 4][:, :], qr[:, par, tile(b)], k_lo[:, par, b, :, :], start=False,
                                  stop=True).then_inc(s_score, 1)
                    if 2 <= n < UNITS + 2:
                        m = n - 2
                        pe.wait_ge(s_exp, nth(UNITS, g, m))
                        pe.wait_ge(s_pTc, nth(UNITS, g, m - 2))
                        for a in range(REP1):
                            mm = pe.transpose(M.tp[m % 2][:, a * S:(a + 1) * S], prob[:, m % 4, a * S:(a + 1) * S], M.ident[:, :])
                        mm.then_inc(s_pT, 1)
                    if n >= 3:
                        m = n - 3
                        par, b = divmod(m, NB)
                        pe.wait_ge(s_pTc, nth(UNITS, g, m))
                        if m % QUAD == 0:
                            pe.wait_ge(s_att, nth(4, g, m // QUAD - 2))
                        for a in range(REP1):
                            key_head = M.v1[:, b, bass.ds(g * 2 + par, 1), :].rearrange("p j d -> p (j d)")
                            mm = pe.matmul(av[(m // QUAD) % 2][:, m % QUAD, a, :], probT[:, m % 2, a * S:(a + 1) * S],
                                           key_head, start=True, stop=True)
                        mm.then_inc(s_pv, 1)
            for b in range(NB + 1):
                if b < NB:
                    pe.wait_ge(s_att, 4 + KV1 * 2)
                    if b >= 2:
                        pe.wait_ge(s_alo, b - 1)
                    for k in range(KT):
                        mm = pe.transpose(M.pj[b % 2][:, k * P:(k + 1) * P], att[:, b, k * P:(k + 1) * P], M.ident[:, :])
                    mm.then_inc(s_aT, 1)
                if b:
                    c = b - 1
                    pe.wait_ge(s_alo, c + 1)
                    pe.wait_ge(s_w, 4)
                    if c >= 2:
                        pe.wait_ge(s_acc, c - 1)
                    bank = M.pj[2 + c % 2][:, :]
                    for k in range(KT):
                        pe.matmul(bank, M.xT_hi[:, k, tile(c)], w_hi[:, k, :], start=(k == 0), stop=False)
                        pe.matmul(bank, M.xT_hi[:, k, tile(c)], w_lo[:, k, :], start=False, stop=False)
                        mm = pe.matmul(bank, M.xT_lo[:, k, tile(c)], w_hi[:, k, :], start=False, stop=(k == KT - 1))
                    mm.then_inc(s_out, 1)


class LayerNorm:

    def __init__(self, M, sem, tag, xn):
        self.M, self.xn = M, xn
        self.s_stats, self.s_xn, self.s_tr, self.s_hi, self.s_lo = (
            sem(f"s_{tag}_{n}") for n in ("stats", "xn", "transposed", "hi", "lo"))
        self.root = RootSteps(M, sem, tag)

    def vector(self, dve):
        M = self.M
        layernorm_stats(dve, M, self.s_stats, self.root)
        self.root.vector(dve)
        for b in range(NB):
            dve.tensor_scalar(self.xn[:, b, :], M.acc[:, b, :], M.mv[:, b, 0:1], M.rs[:, b:b + 1],
                              ALU.subtract, ALU.mult).then_inc(self.s_xn, 1)
        for b in range(NB):
            at = slice(b * S, (b + 1) * S)
            dve.wait_ge(self.s_hi, b + 1)
            dve.tensor_tensor(M.xT_lo[:, :, at], M.pj[b % 4][:, :].rearrange("p (k s) -> p k s", k=KT),
                              M.xT_hi[:, :, at], ALU.subtract).then_inc(self.s_lo, 1)

    def scalar(self, act):
        M = self.M
        self.root.scalar(act)
        for b in range(NB):
            act.wait_ge(self.s_tr, b + 1)
            act.activation(M.xT_hi[:, :, b * S:(b + 1) * S], M.pj[b % 4][:, :].rearrange("p (k s) -> p k s", k=KT),
                           ACT.Copy).then_inc(self.s_hi, 1)

    def tensor(self, pe):
        M = self.M
        for b in range(NB):
            pe.wait_ge(self.s_xn, b + 1)
            if b >= 4:
                pe.wait_ge(self.s_lo, b - 3)
            for k in range(KT):
                mm = pe.transpose(M.pj[b % 4][:, k * P:(k + 1) * P], self.xn[:, b, k * P:(k + 1) * P], M.ident[:, :])
            mm.then_inc(self.s_tr, 1)
        pe.wait_ge(self.s_lo, NB)


def of_tile(per_tile, t, i):
    return (t + 2) * per_tile + (i + 1)


GATE, UP, DOWN = range(3)
LOOPED = FT - 3


def ffn_phase(nc, M, sb, sem, layer, gq, gs, gz, nibble_shift):
    L = f"f{layer}"
    s_in = [[sem(f"s_{L}_in{p}{u}") for u in range(3)] for p in range(2)]
    s_unit = sem(f"s_{L}_unit")
    s_hi = sem(f"s_{L}_hi")
    s_lo = sem(f"s_{L}_lo")
    s_gu = sem(f"s_{L}_gate_up")
    s_silu = sem(f"s_{L}_silu")
    s_h = sem(f"s_{L}_h")
    s_ints = sem(f"s_{L}_ints")
    s_hs_hi = sem(f"s_{L}_hs_hi")
    s_hs_lo = sem(f"s_{L}_hs_lo")
    s_down = sem(f"s_{L}_down")
    s_acc = sem(f"s_{L}_acc")
    s_zero = sem(f"s_{L}_zero")
    s_shift = sem(f"s_{L}_shift")
    half = lambda j: slice(j * HALF, (j + 1) * HALF)
    tile = lambda b: slice(b * S, (b + 1) * S)
    gain = M.tg[:, 2 + layer:3 + layer]

    with ExitStack() as local:
        hT = sb(f"hT{layer}", [P, FT, TOK], F32, local)
        dn_hi = sb(f"dn_hi{layer}", [P, FT, D], F32R, local)
        dn_lo = sb(f"dn_lo{layer}", [P, FT, D], F32R, local)
        wT_hi = sb(f"wT_hi{layer}", [P, 2, 2, D], F32R, local)
        wT_lo = sb(f"wT_lo{layer}", [P, 2, 2, D], F32R, local)
        silu = sb(f"silu{layer}", [P, 2, HALF], F32, local)
        raw = sb(f"raw{layer}", [P, 2, 3, D], I32 if layer else F32, local)
        if layer:
            scale = sb("scale", [P, 2, 3, D], F16, local)
            zwords = sb("zwords", [P, 2, 3, D // 8], I32, local)
            nibs = sb("nibs", [P, 2, D], I32, local)
            zeros = sb("zeros", [P, 2, D], I32, local)
            ints = sb("ints", [P, 2, D], F32, local)
            unit_f = sb("unit_f", [P, 2, D], F32, local)
            shift = sb("shift", [P, 1], I32, local)
            ffn_out = sb("ffn_out", [P, 2, D], F16, local)
        ln = LayerNorm(M, sem, f"{L}_ln", hT[:, 0:NB * D // TOK, :].rearrange("p a (b d) -> p (a b) d", d=D))
        split_cols = FT * S
        flat = lambda t: t[:, :, :].rearrange("p k n -> p (k n)")
        hs_hi, hs_lo = ([flat(t)[:, i * split_cols:(i + 1) * split_cols].rearrange("p (f s) -> p f s", s=S)
                         for i in range(2)] for t in (M.xT_hi, M.xT_lo))
        block = local.enter_context(nc.Block())

        def over_tiles(eng, prepare, consume):
            prepare(0, 0)
            with eng.Fori(0, LOOPED // 2) as g:
                for par in range(2):
                    prepare(g * 2 + (par + 1), (par + 1) % 2)
                    consume(g * 2 + par, par)
            for t in range(LOOPED, FT):
                if t + 1 < FT:
                    prepare(t + 1, (t + 1) % 2)
                consume(t, t % 2)

        last_tile = lambda t: isinstance(t, int) and t == FT - 1
        rows_of = lambda t, u: FREST if layer == 0 and u == DOWN and last_tile(t) else P
        banks = [M.tp[0], M.tp[1], M.sc[0]]

        if layer == 0:
            flat_dq = M.nf4_dq.rearrange("p n -> (p n)")
            w1, w2 = (flat_dq[i * FPAD * D:(i + 1) * FPAD * D].rearrange("(t p n) -> t p n", t=FT, n=D) for i in range(2))
            w3 = flat_dq[2 * FPAD * D:].rearrange("(k p n) -> p k n", k=KT, n=FF)

        @block.sync
        def _(sp):
            def load(t, par):
                for u in range(3):
                    sp.wait_ge(s_unit, of_tile(3, t - 2, u))
                    if layer:
                        sp.dma_start(raw[:, par, u, :], gq[t, u]).then_inc(s_in[par][u], 16)
                        sp.dma_start(scale[:, par, u, :], gs[t, u].partition_broadcast(P)).then_inc(s_in[par][u], 16)
                        sp.dma_start(zwords[:, par, u, :], gz[t, u].partition_broadcast(P)).then_inc(s_in[par][u], 16)
                    elif u < DOWN:
                        sp.dma_start(raw[:, par, u, :], (w1, w2)[u][t]).then_inc(s_in[par][u], 16)
                    else:
                        n = rows_of(t, u)
                        at = slice(t * P, t * P + n) if isinstance(t, int) else bass.ts(t, P)
                        sp.dma_start(raw[:, par, u, :].rearrange("p (k h) -> p k h", k=KT)[:, :, 0:n],
                                     w3[:, :, at]).then_inc(s_in[par][u], 16)

            if layer:
                sp.dma_start(shift[:, :], nibble_shift).then_inc(s_shift, 16)
            over_tiles(sp, load, lambda t, par: None)

        arrivals = 48 if layer else 16
        arrived = lambda t, par: (t - par) * (arrivals // 2) + arrivals

        @block.gpsimd
        def _(pool):
            if layer:
                pool.sem_inc(s_unit, 6)

                def scale_unit(t, par):
                    for u in range(3):
                        i = (par * 3 + u) % 2
                        pool.wait_ge(s_lo, of_tile(3, t, u - 2))
                        pool.wait_ge(s_ints, of_tile(9, t, 3 * u + 2))
                        pool.tensor_tensor(unit_f[:, i, :], ints[:, i, :], scale[:, par, u, :],
                                           ALU.mult).then_inc(s_unit, 1)

                over_tiles(pool, scale_unit, lambda t, par: None)
            for b in range(NB):
                pool.wait_ge(s_h, of_tile(2, FT - 1, 1))
                if b >= 2:
                    pool.wait_ge(s_down, b - 1)
                pool.tensor_copy(hs_hi[b % 2], hT[:, :, tile(b)]).then_inc(s_hs_hi, 1)

        @block.scalar
        def _(act):
            act.sem_inc(s_hi, 6)
            act.sem_inc(s_silu, 4)
            ln.scalar(act)

            def high(t, par):
                for u in range(3):
                    n = rows_of(t, u)
                    act.wait_ge(s_gu, of_tile(4, t - 2, 3))
                    act.wait_ge(s_unit, of_tile(3, t, u))
                    if u == DOWN:
                        dst = dn_hi[0:n, t, :]
                        src = unit_f[:, (par * 3 + u) % 2, :] if layer else banks[u][0:n, :]
                    else:
                        dst = wT_hi[:, par, u, :]
                        src = unit_f[:, (par * 3 + u) % 2, :] if layer else banks[u][:, :]
                    act.activation(dst, src, ACT.Copy).then_inc(s_hi, 1)

            def silus(t, par):
                for j in range(2):
                    act.wait_ge(s_gu, of_tile(4, t, 2 * j))
                    act.activation(silu[:, j, :], M.pj[2 * j][:, :], ACT.Silu).then_inc(s_silu, 1)

            over_tiles(act, high, silus)

        @block.vector
        def _(dve):
            dve.sem_inc(s_lo, 6)
            dve.sem_inc(s_h, 4)
            dve.sem_inc(s_ints, 18)
            if layer == 0:
                dve.memset(dn_lo[FREST:P, FT - 1, :].bitcast(F32), 0.0).then_inc(s_zero, 1)
                dve.memset(dn_hi[FREST:P, FT - 1, :].bitcast(F32), 0.0).then_inc(s_zero, 1)
            ln.vector(dve)

            def unpack(t, par, u):
                i = (par * 3 + u) % 2
                dve.wait_ge(s_in[par][u], arrived(t, par))
                dve.wait_ge(s_shift, 16)
                dve.wait_ge(s_ints, of_tile(9, t, 3 * (u - 2) + 2))
                dve.tensor_scalar(nibs[:, i, :], raw[:, par, u, :], shift[:, 0:1], 15, ALU.logical_shift_right,
                                  ALU.bitwise_and).then_inc(s_ints, 1)
                z = zeros[:, i, :].rearrange("p (n e) -> p n e", e=8)
                for e in range(8):
                    last = dve.tensor_scalar(z[:, :, e], zwords[:, par, u, :], 4 * e, 15, ALU.logical_shift_right,
                                             ALU.bitwise_and)
                last.then_inc(s_ints, 1)
                dve.wait_ge(s_unit, of_tile(3, t, u - 2))
                dve.wait_ge(s_ints, of_tile(9, t, 3 * u + 1))
                dve.scalar_tensor_tensor(ints[:, i, :], nibs[:, i, :], 1.0, zeros[:, i, :], op0=ALU.subtract,
                                         op1=ALU.subtract).then_inc(s_ints, 1)

            def low(t, par, u):
                n = rows_of(t, u)
                dve.wait_ge(s_hi, of_tile(3, t, u))
                src = unit_f[0:n, (par * 3 + u) % 2, :] if layer else banks[u][0:n, :]
                hi = dn_hi[0:n, t, :] if u == DOWN else wT_hi[:, par, u, :]
                lo = dn_lo[0:n, t, :] if u == DOWN else wT_lo[:, par, u, :]
                dve.tensor_tensor(lo, src, hi, ALU.subtract).then_inc(s_lo, 1)

            def prepare(t, par):
                if layer:
                    unpack(t, par, GATE)
                    unpack(t, par, UP)
                    low(t, par, GATE)
                    unpack(t, par, DOWN)
                    low(t, par, UP)
                    low(t, par, DOWN)
                else:
                    for u in range(3):
                        low(t, par, u)

            def hidden(t, par):
                for j in range(2):
                    dve.wait_ge(s_silu, of_tile(2, t, j))
                    dve.wait_ge(s_gu, of_tile(4, t, 2 * j + 1))
                    dve.tensor_tensor(hT[:, t, half(j)], M.pj[2 * j + 1][:, :], silu[:, j, :],
                                      ALU.mult).then_inc(s_h, 1)

            over_tiles(dve, prepare, hidden)

            def split(b):
                dve.wait_ge(s_hs_hi, b + 1)
                dve.tensor_tensor(hs_lo[b % 2], hT[:, :, tile(b)], hs_hi[b % 2], ALU.subtract).then_inc(s_hs_lo, 1)

            split(0)
            split(1)
            for b in range(NB):
                dve.wait_ge(s_down, b + 1)
                out = M.pj[b % 4][:, :]
                if layer:
                    dve.tensor_copy(ffn_out[:, b % 2, :], out).then_inc(s_zero, 1)
                    dve.wait_ge(s_zero, b + 1)
                    out = ffn_out[:, b % 2, :]
                dve.scalar_tensor_tensor(M.acc[:, b, :], out, gain, M.acc[:, b, :], op0=ALU.mult,
                                         op1=ALU.add).then_inc(s_acc, 1)
                if b + 2 < NB:
                    split(b + 2)
            dve.wait_ge(s_acc, NB)

        @block.tensor
        def _(pe):
            pe.sem_inc(s_gu, 8)
            if layer == 0:
                pe.sem_inc(s_unit, 6)

            def transposes(t, par):
                if layer:
                    return
                for u in range(3):
                    n = rows_of(t, u)
                    pe.wait_ge(s_in[par][u], arrived(t, par))
                    pe.wait_ge(s_lo, of_tile(3, t - 1, u))
                    for k in range(KT):
                        mm = pe.transpose(banks[u][0:n, k * P:(k + 1) * P], raw[:, par, u, k * P:k * P + n],
                                          M.ident[:, :])
                    mm.then_inc(s_unit, 1)

            def products(t, par):
                for j in range(2):
                    for u in (GATE, UP):
                        bank = M.pj[2 * j + u][:, :]
                        pe.wait_ge(s_h, of_tile(2, t - 1, j))
                        if j == 0:
                            pe.wait_ge(s_lo, of_tile(3, t, u))
                        for k in range(KT):
                            w = slice(k * P, (k + 1) * P)
                            hi, lo = wT_hi[:, par, u, w], wT_lo[:, par, u, w]
                            pe.matmul(bank, hi, M.xT_hi[:, k, half(j)], start=(k == 0), stop=False)
                            pe.matmul(bank, hi, M.xT_lo[:, k, half(j)], start=False, stop=False)
                            mm = pe.matmul(bank, lo, M.xT_hi[:, k, half(j)], start=False, stop=(k == KT - 1))
                        mm.then_inc(s_gu, 1)

            ln.tensor(pe)
            over_tiles(pe, transposes, products)
            for b in range(NB):
                bank = M.pj[b % 4][:, :]
                pe.wait_ge(s_hs_lo, b + 1)
                if b == 0:
                    pe.wait_ge(s_lo, of_tile(3, FT - 1, DOWN))
                    if layer == 0:
                        pe.wait_ge(s_zero, 2)
                if b >= 4:
                    pe.wait_ge(s_acc, b - 3)
                for t in range(FT):
                    pe.matmul(bank, hs_hi[b % 2][:, t, :], dn_hi[:, t, :], start=(t == 0), stop=False)
                    pe.matmul(bank, hs_hi[b % 2][:, t, :], dn_lo[:, t, :], start=False, stop=False)
                    mm = pe.matmul(bank, hs_lo[b % 2][:, t, :], dn_hi[:, t, :], start=False, stop=(t == FT - 1))
                mm.then_inc(s_down, 1)


_OUT = ((NB, S, D), "float32")


def kernel(**inputs):
    import concourse.bacc as bacc
    from concourse.bass_utils import run_bass_kernel_spmd

    a = {k: np.asarray(v) for k, v in inputs.items()}
    by_head = lambda w: w.reshape(H0, DH0, KT, P).transpose(0, 3, 2, 1)
    pad = ((0, FPAD - FF), (0, 0))
    nf4 = np.concatenate([np.pad(a["L0_ffn_w1"], pad).reshape(-1), np.pad(a["L0_ffn_w2"], pad).reshape(-1),
                          a["L0_ffn_w3"].reshape(-1)])

    g = {k[7:]: v for k, v in a.items() if k.startswith("L1_ffn_")}
    padded = lambda w, rows, cols: np.pad(w, ((0, rows - w.shape[0]), (0, cols - w.shape[1])))
    by_tile = lambda w: np.moveaxis(w.reshape(*w.shape[:-1], FT, -1), -2, 0)
    across = lambda w: by_tile(w).reshape(FT, -1)
    words = lambda w, rows, cols: np.repeat(padded(w, rows // 8, cols), 8, axis=0)
    wide = lambda w: by_tile(words(w, D, FPAD).reshape(KT, P, FPAD).transpose(1, 0, 2)).reshape(FT, P, D)
    gq = np.stack([wide(g["gate_qweight"]), wide(g["up_qweight"]),
                   words(g["down_qweight"], FPAD, D).reshape(FT, P, D)], 1)
    gs = np.stack([across(padded(g["gate_scales"], KT, FPAD)), across(padded(g["up_scales"], KT, FPAD)),
                   g["down_scales"]], 1)
    gz = np.stack([across(padded(g["gate_zeros"], KT, FPAD // 8)), across(padded(g["up_zeros"], KT, FPAD // 8)),
                   g["down_zeros"]], 1)
    arrays = {
        "x": a["x"], "ctx_in": a["ctx_4096"], "mask": np.ascontiguousarray(a["mask_BxSxS2_bk0"]).view(np.int32),
        "gains": np.concatenate([a["g_xattn"], a["g_ffn"]]), "lnw": a["L0_xattn_ln_weight"],
        "pbias": a["L0_xattn_position_bias"].reshape(GROUPS, GH, S, S).transpose(0, 2, 1, 3),
        "wqk0": np.pad(np.stack([by_head(a["L0_xattn_w_q"]), by_head(a["L0_xattn_w_k"])], 2).reshape(H0, P, 2 * KT * DH0), ((0, 1), (0, 0), (0, 0))),
        "wv0": np.pad(a["L0_xattn_w_v"].reshape(GROUPS, GH * DH0, KT, P).transpose(0, 2, 3, 1), ((0, 1), (0, 0), (0, 0), (0, 0))),
        "wo0": a["L0_xattn_w_out"].T.reshape(H0, P, D),
        "nf4_src": nf4.reshape(P, NFW), "gq": gq, "gs": gs, "gz": gz,
        "wkv1": np.stack([a[f"L1_xattn_W{m}"].reshape(KT, P, P).transpose(1, 0, 2).reshape(P, KT * P) for m in "kv"], 1),
        "wq1": a["L1_xattn_Wq"].reshape(KT, P, D).transpose(1, 0, 2), "wo1": a["L1_xattn_Wo"].reshape(KT, P, D).transpose(1, 0, 2),
        "nibble_shift": (4 * (np.arange(P, dtype=np.int32) % 8)).reshape(P, 1),
    }
    arrays = {k: np.ascontiguousarray(v) for k, v in arrays.items()}
    nc = bacc.Bacc("TRN2", target_bir_lowering=False, num_devices=1, dynamic_dma_scratch_size=8192)
    aps = {k: nc.dram_tensor(f"in_{k}", v.shape, mybir.dt.from_np(v.dtype), kind="ExternalInput").ap()
           for k, v in arrays.items()}
    out = nc.dram_tensor("out_dram", _OUT[0], F32, kind="ExternalOutput").ap()
    flamingo(nc, **aps, out=out)
    r = run_bass_kernel_spmd(nc, [{f"in_{k}": v for k, v in arrays.items()}], core_ids=[0])
    return r.results[0]["out_dram"]
```

```python
from contextlib import ExitStack

import numpy as np

import concourse.bass as bass
from concourse import mybir

F32 = mybir.dt.float32
F32R = mybir.dt.float32r
BF16 = mybir.dt.bfloat16
F16 = mybir.dt.float16
I32 = mybir.dt.int32
U8 = mybir.dt.uint8
ALU = mybir.AluOpType
ACT = mybir.ActivationFunctionType
AX = mybir.AxisListType

P = 128
NB = 8
S = 128
TOK = NB * S
D = 512
KT = D // P
H0, DH0 = 32, 128
GH = 4
GROUPS = H0 // GH
HALF = 512
QUAD = HALF // S
H1, KV1, DH1 = 32, 8, 16
REP1 = H1 // KV1
FF = 1376
FT = -(-FF // P)
FPAD = FT * P
FREST = FF - (FT - 1) * P
EPS = 1e-5
MASKED = -1e30

NF4_CODE = np.array(
    [-1.0, -0.6961928009986877, -0.5250730514526367, -0.39491748809814453, -0.28444138169288635,
     -0.18477343022823334, -0.09105003625154495, 0.0, 0.07958029955625534, 0.16093020141124725,
     0.24611230194568634, 0.33791524171829224, 0.44070982933044434, 0.5626170039176941,
     0.7229568362236023, 1.0], dtype=np.float32)
NF4_BOUNDS = ((NF4_CODE[:-1] + NF4_CODE[1:]) * np.float32(0.5)).astype(np.float32)
NLEV = len(NF4_BOUNDS)
QB = 64
NFW = (2 * FPAD + FF) * D // P
NFC = 512
NFTAIL = NFW - H0 * NFC


def nth(per_group, g, n):
    assert -per_group <= n < per_group
    return g * per_group + (per_group + n + 1)


class Shared:
    pass


def flamingo(nc, x, ctx_in, mask, gains, lnw, pbias, wqk0, wv0, wo0, nf4_src, gq, gs, gz, nibble_shift, wkv1, wq1, wo1, out):
    stack = ExitStack()
    with stack:
        M = Shared()
        sb = lambda name, shape, dt, where=stack: where.enter_context(nc.sbuf_tensor(name, shape, dt))
        pb = lambda name: stack.enter_context(nc.psum_tensor(name, [P, HALF], F32))

        sems = []

        def sem(name):
            sems.append(nc.alloc_semaphore(name))
            return sems[-1]

        def phase(run, *args):
            run(nc, M, sb, sem, *args)

        M.acc = sb("acc", [P, NB, D], F32)
        M.xT_hi = sb("xT_hi", [P, KT, TOK], F32R)
        M.xT_lo = sb("xT_lo", [P, KT, TOK], F32R)
        M.ident = sb("ident", [P, P], F32)
        M.ident_b = sb("ident_b", [P, P], BF16)
        M.tg = sb("tg", [P, 4], F32)
        M.stats = sb("stats", [P, NB, 6], F32)
        M.mv = sb("mv", [P, NB, 2], F32)
        M.ve = sb("ve", [P, NB], F32)
        M.sd = sb("sd", [P, NB], F32)
        M.rs = sb("rs", [P, NB], F32)
        M.nt = sb("nt", [P, NB], F32)
        M.pj = [pb(f"pj{i}") for i in range(4)]
        M.sc = [pb(f"sc{i}") for i in range(2)]
        M.tp = [pb(f"tp{i}") for i in range(2)]
        M.v1 = sb("v1", [P, NB, KV1, DH1], F32)
        M.k1_rows = nc.dram_tensor("k1_rows", [2, KV1, DH1, TOK], F32, kind="Internal").ap()
        M.k1_dram = nc.dram_tensor("k1_dram", [2, KV1, 2, DH1, TOK], F32, kind="Internal").ap()
        M.nf4_dq = nc.dram_tensor("nf4_dq", [P, NFW], F32, kind="Internal").ap()

        with ExitStack() as with_context:
            M.cT_hi = sb("cT_hi", [P, KT, TOK], F32R, with_context)
            M.cT_lo = sb("cT_lo", [P, KT, TOK], F32R, with_context)
            M.maskneg = sb("maskneg", [P, TOK], BF16, with_context)
            M.rowany = sb("rowany", [P, NB], F32, with_context)
            M.qk_hi = sb("qk_hi", [P, 2, KT * DH0], F32R, with_context)
            M.qk_lo = sb("qk_lo", [P, 2, KT * DH0], F32R, with_context)
            M.v_hi = sb("v_hi", [P, KT, GH * DH0], F32R, with_context)
            M.v_lo = sb("v_lo", [P, KT, GH * DH0], F32R, with_context)
            phase(setup_phase, x, ctx_in, mask, gains, lnw, wkv1, wqk0, wv0)
            phase(attention0_phase, pbias, wqk0, wv0, wo0, nf4_src)
        nc.clear_and_free_semaphores(sems)
        nc.all_engine_barrier()
        M.w_raw = sb("w1_raw", [P, KT, D], F32)
        M.s_wraw = [sem(f"s_a1_wraw{k}") for k in range(KT)]
        phase(ffn_phase, 0, wq1)
        M.raw_first = sb("raw1_first", [P, 3, D], I32)
        M.scale_first = sb("scale_first", [P, 3, D], F16)
        M.zwords_first = sb("zwords_first", [P, 3, D // 8], I32)
        M.shift = sb("shift", [P, 1], I32)
        M.s_first_in = [sem(f"s_f1_in0{u}") for u in range(3)]
        M.s_shift = sem("s_f1_shift")
        phase(attention1_phase, wo1, gq, gs, gz, nibble_shift)
        phase(ffn_phase, 1, None, gq, gs, gz, out)


class RootSteps:

    def __init__(self, M, sem, tag):
        self.M = M
        self.asked = sem(f"s_{tag}_ve")
        self.rooted = sem(f"s_{tag}_root")
        self.step = sem(f"s_{tag}_newton")

    def scalar(self, act):
        act.wait_ge(self.asked, 1)
        act.activation(self.M.sd[:, :], self.M.ve[:, :], ACT.Sqrt).then_inc(self.rooted, 1)

    def vector(self, dve):
        M = self.M
        dve.wait_ge(self.rooted, 1)
        dve.reciprocal(M.rs[:, :], M.sd[:, :]).then_inc(self.step, 1)
        dve.wait_ge(self.step, 1)
        dve.tensor_tensor(M.nt[:, :], M.rs[:, :], M.rs[:, :], ALU.mult).then_inc(self.step, 1)
        dve.wait_ge(self.step, 2)
        dve.tensor_tensor(M.nt[:, :], M.nt[:, :], M.ve[:, :], ALU.mult).then_inc(self.step, 1)
        dve.wait_ge(self.step, 3)
        dve.tensor_scalar(M.nt[:, :], M.nt[:, :], -0.5, 1.5, ALU.mult, ALU.add).then_inc(self.step, 1)
        dve.wait_ge(self.step, 4)
        dve.tensor_tensor(M.rs[:, :], M.rs[:, :], M.nt[:, :], ALU.mult).then_inc(self.step, 1)
        dve.wait_ge(self.step, 5)


def layernorm_stats(dve, M, s_stats, root):
    for b in range(NB):
        dve.bn_stats(M.stats[:, b, :], M.acc[:, b, :]).then_inc(s_stats, 1)
    for b in range(NB):
        dve.wait_ge(s_stats, b + 1)
        dve.bn_aggr(M.mv[:, b, :], M.stats[:, b, :]).then_inc(s_stats, 1)
    dve.wait_ge(s_stats, 2 * NB)
    dve.tensor_scalar(M.ve[:, :], M.mv[:, :, 1], EPS, None, ALU.add).then_inc(root.asked, 1)


def nf4_prepare(dve, chain, done, raw, norm, absmax, recip, width):
    blocks = width // QB
    cut = lambda t: t[:, 0:width].rearrange("p (n q) -> p n q", q=QB)
    dve.tensor_reduce(absmax[:, 0:blocks], cut(raw), AX.X, ALU.max, apply_absolute_value=True).then_inc(chain, 1)
    dve.wait_ge(chain, done(0))
    dve.scalar_tensor_tensor(recip[:, 0:blocks], absmax[:, 0:blocks], 0.0, absmax[:, 0:blocks],
                             op0=ALU.is_equal, op1=ALU.add).then_inc(chain, 1)
    dve.wait_ge(chain, done(1))
    dve.reciprocal(recip[:, 0:blocks], recip[:, 0:blocks]).then_inc(chain, 1)
    dve.wait_ge(chain, done(2))
    dve.tensor_tensor(cut(norm), cut(raw), recip[:, 0:blocks].unsqueeze(2).broadcast_to([P, blocks, QB]),
                      ALU.mult).then_inc(chain, 1)


def nf4_threshold(k):
    b = NF4_BOUNDS[k]
    return float(np.nextafter(b, np.float32(2.0))) if NF4_CODE[k + 1] <= 0 else float(b)


def nf4_level(dve, k, sign, code):
    if k == 0:
        return dve.tensor_scalar(code, sign, float(NF4_CODE[1]), float(NF4_CODE[0]), ALU.min, ALU.max)
    return dve.scalar_tensor_tensor(code, sign, float(NF4_CODE[k + 1]), code, op0=ALU.min, op1=ALU.max)


def nf4_finish(dve, raw, code, absmax, width):
    blocks = width // QB
    cut = lambda t: t[:, 0:width].rearrange("p (n q) -> p n q", q=QB)
    return dve.tensor_tensor(cut(raw), cut(code), absmax[:, 0:blocks].unsqueeze(2).broadcast_to([P, blocks, QB]),
                             ALU.mult)


def setup_phase(nc, M, sb, sem, x, ctx_in, mask, gains, lnw, wkv1, wqk0, wv0):
    s_x = [sem(f"s_in_x{b}") for b in range(NB)]
    s_c = [sem(f"s_in_ctx{b}") for b in range(NB)]
    s_m, s_g, s_l, s_w = (sem(f"s_in_{n}") for n in ("mask", "gains", "lnw", "wkv1"))
    s_id = sem("s_ident")
    s_tg = sem("s_tanh")
    s_maskf = sem("s_maskf")
    s_stats = sem("s_ln0_stats")
    s_ms = sem("s_mean_square")
    s_x1 = sem("s_x1")
    s_acc = sem("s_acc_start")
    s_gx = sem("s_gated_x1")
    s_xn = sem("s_xn")
    s_wsplit = sem("s_wkv1_split")
    s_tr = sem("s_setup_transposed")
    s_hi = sem("s_setup_hi")
    s_lo = sem("s_setup_lo")
    s_kv = sem("s_kv1")
    s_k1 = sem("s_k1_hi")
    s_k1lo = sem("s_k1_lo")
    s_v1T = sem("s_v1T")
    s_v1 = sem("s_v1")
    s_kout = sem("s_k1_out")
    ln_root = RootSteps(M, sem, "ln0")
    rms_root = RootSteps(M, sem, "rms")
    s_in_first = [sem(f"s_in_first{i}") for i in range(KT + 2)]
    s_first_hi = sem("s_first_hi")
    s_first_lo = sem("s_first_lo")
    s_first_vlo = sem("s_first_vlo")
    half = lambda j: slice(j * HALF, (j + 1) * HALF)

    with ExitStack() as local:
        c_nat = sb("c_nat", [P, NB, D], F32, local)
        x1 = sb("x1", [P, NB, D], F32, local)
        xn = sb("xn", [P, NB, D], F32, local)
        square = sb("square", [P, D], F32, local)
        gated = sb("gated", [P, NB, D], F32, local)
        mean_sq = sb("mean_sq", [P, NB], F32, local)
        lnw_b = sb("lnw_b", [P, D], F32, local)
        mask_words = sb("mask_words", [P, TOK // 4], I32, local)
        mask_u8 = mask_words.bitcast(U8)
        g_sb = sb("g_sb", [P, 4], F32, local)
        wkv = sb("wkv", [P, 2, KT * P], F32, local)
        wkv_hi = sb("wkv_hi", [P, 2, KT * P], F32R, local)
        wkv_lo = sb("wkv_lo", [P, 2, KT * P], F32R, local)
        k1_hi = sb("k1_hi", [P, TOK], F32R, local)
        k1_lo = sb("k1_lo", [P, TOK], F32R, local)
        v1T = sb("v1T", [P, TOK], F32, local)
        first = ([(M.v_hi[:, i, :], M.v_lo[:, i, :], c_nat[:, i, :], wv0[0, i]) for i in range(KT)]
                 + [(M.qk_hi[:, m, :], M.qk_lo[:, m, :], c_nat[:, KT + m, :], wqk0[0][:, m * KT * DH0:(m + 1) * KT * DH0])
                    for m in range(2)])
        block = local.enter_context(nc.Block())
        by_k = lambda bank: bank[:, :].rearrange("p (k s) -> p k s", k=KT)

        @block.sync
        def _(sp):
            for b in range(NB):
                sp.dma_start(M.acc[:, b, :], x[b]).then_inc(s_x[b], 16)
            for b in range(NB):
                sp.dma_start(c_nat[:, b, :], ctx_in[b]).then_inc(s_c[b], 16)
            sp.dma_start(wkv[:, :, :], wkv1).then_inc(s_w, 16)
            sp.wait_ge(s_tr, NB)
            for n, (_, _, raw, src) in enumerate(first):
                sp.dma_start(raw, src).then_inc(s_in_first[n], 16)
            sp.wait_ge(s_k1lo, 2)
            for part, src in enumerate((k1_hi, k1_lo)):
                sp.dma_start(M.k1_rows[part].rearrange("h d t -> (h d) t"), src[:, :].bitcast(F32)).then_inc(s_kout, 16)
            sp.wait_ge(s_kout, 16 * 2)

        @block.gpsimd
        def _(pool):
            pool.memset(M.ident[:, :], 0.0).then_inc(s_id, 1)
            pool.memset(M.ident_b[:, :], 0.0).then_inc(s_id, 1)
            pool.wait_ge(s_id, 2)
            for t in (M.ident, M.ident_b):
                pool.affine_select(out=t[:, :], in_=t[:, :], compare_op=ALU.not_equal, fill=1.0, base=0,
                                   pattern=[[-1, P]], channel_multiplier=1).then_inc(s_id, 1)
            pool.wait_ge(s_w, 16)
            for m in range(2):
                pool.tensor_copy(wkv_hi[:, m, :], wkv[:, m, :]).then_inc(s_id, 1)
                pool.wait_ge(s_id, 5 + m)
                pool.tensor_tensor(wkv_lo[:, m, :], wkv[:, m, :], wkv_hi[:, m, :], ALU.subtract).then_inc(s_wsplit, 1)
            for b in range(NB):
                pool.wait_ge(s_gx, b + 1)
                pool.tensor_tensor(M.acc[:, b, :], gated[:, b, :], M.acc[:, b, :], ALU.add).then_inc(s_acc, 1)
            for n in range(KT):
                pool.wait_ge(s_first_hi, n + 1)
                pool.tensor_tensor(first[n][1], first[n][2], first[n][0], ALU.subtract).then_inc(s_first_vlo, 1)

        @block.scalar
        def _(act):
            act.dma_start(g_sb[:, :], gains.partition_broadcast(P)).then_inc(s_g, 16)
            act.dma_start(mask_words[:, :].rearrange("p (b k) -> p b k", b=NB),
                          mask.rearrange("b q k -> q b k")).then_inc(s_m, 16)
            act.dma_start(lnw_b[:, :], lnw.partition_broadcast(P)).then_inc(s_l, 16)
            act.wait_ge(s_g, 16)
            act.activation(M.tg[:, :], g_sb[:, :], ACT.Tanh).then_inc(s_tg, 1)

            def context_high(b):
                act.wait_ge(s_tr, b + 1)
                act.activation(M.cT_hi[:, :, b * S:(b + 1) * S], by_k(M.pj[b % 4]), ACT.Copy).then_inc(s_hi, 1)

            ln_root.scalar(act)
            context_high(0)
            for b in range(NB):
                act.wait_ge(s_x1, b + 1)
                if b:
                    act.wait_ge(s_ms, b)
                act.activation(square[:, :], x1[:, b, :], ACT.Square,
                               accum_out=mean_sq[:, b:b + 1]).then_inc(s_ms, 1)
                if b + 1 < NB:
                    context_high(b + 1)
            rms_root.scalar(act)
            act.wait_ge(s_tg, 1)
            for b in range(NB):
                act.activation(gated[:, b, :], x1[:, b, :], ACT.Copy, scale=M.tg[:, 0:1]).then_inc(s_gx, 1)
            for j in range(2):
                act.wait_ge(s_kv, j + 1)
                act.activation(k1_hi[:, half(j)], M.sc[j][:, :], ACT.Copy).then_inc(s_k1, 1)
            for b in range(NB):
                act.wait_ge(s_tr, NB + b + 1)
                act.activation(M.xT_hi[:, :, b * S:(b + 1) * S], by_k(M.pj[b % 4]), ACT.Copy).then_inc(s_hi, 1)
                if b < len(first):
                    act.wait_ge(s_in_first[b], 16)
                    act.activation(first[b][0], first[b][2], ACT.Copy).then_inc(s_first_hi, 1)
            for j in range(2):
                act.wait_ge(s_kv, j + 3)
                act.activation(v1T[:, half(j)], M.tp[j][:, :], ACT.Copy).then_inc(s_v1T, 1)

        @block.vector
        def _(dve):
            def low(t):
                hi, lo, b = ((M.cT_hi, M.cT_lo, t) if t < NB else (M.xT_hi, M.xT_lo, t - NB))
                at = slice(b * S, (b + 1) * S)
                dve.wait_ge(s_hi, t + 1)
                dve.tensor_tensor(lo[:, :, at], by_k(M.pj[t % 4]), hi[:, :, at], ALU.subtract).then_inc(s_lo, 1)

            for b in range(NB):
                dve.wait_ge(s_x[b], 16)
                dve.bn_stats(M.stats[:, b, :], M.acc[:, b, :]).then_inc(s_stats, 1)
            for b in range(NB):
                dve.wait_ge(s_stats, b + 1)
                dve.bn_aggr(M.mv[:, b, :], M.stats[:, b, :]).then_inc(s_stats, 1)
            dve.wait_ge(s_stats, 2 * NB)
            dve.tensor_scalar(M.ve[:, :], M.mv[:, :, 1], EPS, None, ALU.add).then_inc(ln_root.asked, 1)
            ln_root.vector(dve)
            for b in range(NB):
                dve.tensor_scalar(x1[:, b, :], M.acc[:, b, :], M.mv[:, b, 0:1], M.rs[:, b:b + 1],
                                  ALU.subtract, ALU.mult).then_inc(s_x1, 1)
                low(b)
            dve.wait_ge(s_ms, NB)
            dve.tensor_scalar(M.ve[:, :], mean_sq[:, :], 1.0 / D, EPS, ALU.mult, ALU.add).then_inc(rms_root.asked, 1)
            rms_root.vector(dve)
            dve.wait_ge(s_l, 16)
            for b in range(NB):
                dve.scalar_tensor_tensor(xn[:, b, :], x1[:, b, :], M.rs[:, b:b + 1], lnw_b[:, :],
                                         op0=ALU.mult, op1=ALU.mult).then_inc(s_xn, 1)
            for j in range(2):
                dve.wait_ge(s_k1, j + 1)
                dve.tensor_tensor(k1_lo[:, half(j)], M.sc[j][:, :], k1_hi[:, half(j)], ALU.subtract).then_inc(s_k1lo, 1)
            for b in range(NB):
                low(NB + b)
                if KT <= b < len(first):
                    dve.wait_ge(s_first_hi, b + 1)
                    dve.tensor_tensor(first[b][1], first[b][2], first[b][0], ALU.subtract).then_inc(s_first_lo, 1)
            dve.wait_ge(s_m, 16)
            dve.tensor_scalar(M.maskneg[:, :], mask_u8[:, :], -1.0, -MASKED, ALU.add, ALU.mult).then_inc(s_maskf, 1)
            dve.tensor_reduce(M.rowany[:, :], mask_u8[:, :].rearrange("p (b k) -> p b k", b=NB), AX.X,
                              ALU.max).then_inc(s_maskf, 1)
            for j in range(2):
                dve.wait_ge(s_kv, j + 5)
                dve.tensor_copy(M.v1[:, QUAD * j:QUAD * (j + 1), :, :].rearrange("p b n d -> p (b n) d"),
                                M.sc[j][:, :].rearrange("p (b d) -> p b d", d=DH1)).then_inc(s_v1, 1)

        @block.tensor
        def _(pe):
            def transposed(t):
                src, b = ((c_nat, t) if t < NB else (xn, t - NB))
                if t < NB:
                    pe.wait_ge(s_c[b], 16)
                else:
                    pe.wait_ge(s_xn, b + 1)
                if t >= 4:
                    pe.wait_ge(s_lo, t - 3)
                for k in range(KT):
                    mm = pe.transpose(M.pj[t % 4][:, k * P:(k + 1) * P], src[:, b, k * P:(k + 1) * P], M.ident[:, :])
                mm.then_inc(s_tr, 1)

            pe.wait_ge(s_id, 4)
            for t in range(NB):
                transposed(t)
            pe.wait_ge(s_lo, NB)
            for n, (m, j) in enumerate(((0, 0), (0, 1), (1, 0), (1, 1))):
                if n == 2:
                    for t in range(NB, 2 * NB):
                        transposed(t)
                bank = (M.sc, M.tp)[m][j][:, :]
                pe.wait_ge(s_wsplit, m + 1)
                for k in range(KT):
                    w = slice(k * P, (k + 1) * P)
                    pe.matmul(bank, wkv_hi[:, m, w], M.cT_hi[:, k, half(j)], start=(k == 0), stop=False)
                    pe.matmul(bank, wkv_hi[:, m, w], M.cT_lo[:, k, half(j)], start=False, stop=False)
                    mm = pe.matmul(bank, wkv_lo[:, m, w], M.cT_hi[:, k, half(j)], start=False, stop=(k == KT - 1))
                mm.then_inc(s_kv, 1)
            for j in range(2):
                pe.wait_ge(s_v1T, j + 1)
                pe.wait_ge(s_k1lo, j + 1)
                for b in range(QUAD):
                    mm = pe.transpose(M.sc[j][:, b * S:(b + 1) * S],
                                      v1T[:, (QUAD * j + b) * S:(QUAD * j + b + 1) * S], M.ident[:, :])
                mm.then_inc(s_kv, 1)


PJ_USES = ([("v", 0, b) for b in range(NB)]
           + [(m, h, half) for h in (1, 2, 3) for m in "qk" for half in (0, 1)]
           + [("o", 0, t) for t in range(NB)]
           + [(m, GH, half) for m in "qk" for half in (0, 1)]
           + [("o", 1, t) for t in range(NB)])
N_PJ = len(PJ_USES)
N_O = 2 * NB
N_EV = N_PJ - N_O
PRIOR_PJ = PJ_USES.index(("q", GH, 0))
SPLITS = [("q", 1), ("k", 1), ("o", 0), ("o", 1), ("q", 2), ("v", 0), ("k", 2), ("v", 1), ("q", 3), ("v", 2), ("k", 3),
          ("v", 3), ("q", GH), ("k", GH), ("o", 2), ("o", 3)]
N_SP = len(SPLITS)
N_NF = GH * NLEV


def attention0_phase(nc, M, sb, sem, pbias, wqk0, wv0, wo0, nf4_src):
    s_raw_qk = [sem(f"s_raw_qk{i}") for i in range(2)]
    s_raw_v = [sem(f"s_raw_v{i}") for i in range(2)]
    s_raw_o = [sem(f"s_raw_o{i}") for i in range(2)]
    s_bias = sem("s_bias")
    s_whi = sem("s_whi")
    s_wlo = sem("s_wlo")
    s_pj = sem("s_pj")
    s_ev = sem("s_ev")
    s_oadd = sem("s_oadd")
    s_score = sem("s_score")
    s_biased = sem("s_biased")
    s_max = sem("s_max")
    s_exp = sem("s_exp")
    s_rsum = sem("s_rsum")
    s_prob = sem("s_prob")
    s_pT = sem("s_pT")
    s_pTc = sem("s_pTc")
    s_pv = sem("s_pv")
    s_ahi = sem("s_ahi")
    s_alo = sem("s_alo")
    s_nin = [sem(f"s_nin{i}") for i in range(GH)]
    s_nout = [sem(f"s_nout0_{i}") for i in range(GH)]
    s_nprep = sem("s_nprep")
    s_nsign = sem("s_nsign")
    s_nlev = sem("s_nlev")
    s_turn = sem("s_turn")
    s_ndq = sem("s_ndq")
    s_ktwice = sem("s_ktwice")
    s_tin, s_tchain, s_tsign, s_tlev = (sem(f"s_tail_{n}") for n in ("in", "chain", "sign", "level"))

    pj_at = {u: n for n, u in enumerate(PJ_USES)}
    o_at = {u: n for n, u in enumerate([u for u in PJ_USES if u[0] == "o"])}
    ev_at = {u: n for n, u in enumerate([u for u in PJ_USES if u[0] != "o"])}
    split_at = {u: n for n, u in enumerate(SPLITS)}
    half = lambda j: slice(j * HALF, (j + 1) * HALF)
    tile = lambda b: slice(b * S, (b + 1) * S)
    in_half = lambda b: slice((b % QUAD) * S, (b % QUAD + 1) * S)

    with ExitStack() as local:
        raw_qk = sb("raw_qk", [P, 2, 2, KT * DH0], F32, local)
        qk_hi, qk_lo, v_hi, v_lo = M.qk_hi, M.qk_lo, M.v_hi, M.v_lo
        raw_v = sb("raw_v", [P, 2, GH * DH0], F32, local)
        raw_o = sb("raw_o", [P, 2, D], F32, local)
        o_hi = sb("o_hi", [P, 2, D], F32R, local)
        o_lo = sb("o_lo", [P, 2, D], F32R, local)
        bias_sb = sb("bias_sb", [P, GH, S], F32, local)
        qT = sb("qT", [P, TOK], F32, local)
        kT = sb("kT", [P, TOK], F32, local)
        V = sb("V", [P, NB, GH * DH0], F32, local)
        prob = sb("prob", [P, 2, TOK], F32, local)
        probT = sb("probT", [P, TOK], F32, local)
        a_hi = sb("a_hi", [P, 3, TOK], F32R, local)
        a_lo = sb("a_lo", [P, 3, TOK], F32R, local)
        nmax = sb("nmax", [P, 2, NB], F32, local)
        rsum = sb("rsum", [P, 2, NB], F32, local)
        nraw = sb("nraw", [P, GH, NFC], F32, local)
        nnorm = sb("nnorm", [P, 2, NFC], F32, local)
        ncode = sb("ncode", [P, NFC], F32, local)
        nsign = sb("nsign", [P, 4, NFC], BF16, local)
        nabs = sb("nabs", [P, 2, NFC // QB], F32, local)
        nrec = sb("nrec", [P, NFC // QB], F32, local)
        tail = slice(H0 * NFC, NFW)
        slot = lambda h: h % 3

        def piece(m, i):
            if m == "v":
                return v_hi[:, i, :], v_lo[:, i, :], raw_v[:, i % 2, :], s_raw_v[i % 2]
            if m == "o":
                return o_hi[:, i % 2, :], o_lo[:, i % 2, :], raw_o[:, i % 2, :], s_raw_o[i % 2]
            mi = "qk".index(m)
            return qk_hi[:, mi, :], qk_lo[:, mi, :], raw_qk[:, i % 2, mi, :], s_raw_qk[i % 2]

        block = local.enter_context(nc.Block())

        @block.sync
        def _(sp):
            def load_qk(g, h):
                sp.wait_ge(s_wlo, nth(N_SP, g, split_at["k", h - 2] if h > 2 else split_at["k", h + 2] - N_SP))
                sp.dma_start(raw_qk[:, h % 2, :, :].rearrange("p m n -> p (m n)"), wqk0[g * GH + h]).then_inc(s_raw_qk[h % 2], 16)

            def load_o(g, h):
                sp.wait_ge(s_wlo, nth(N_SP, g, split_at["o", h - 2] if h >= 2 else split_at["o", h + 2] - N_SP))
                sp.dma_start(raw_o[:, h % 2, :], wo0[g * GH + h]).then_inc(s_raw_o[h % 2], 16)

            def load_v(g, i):
                sp.wait_ge(s_wlo, nth(N_SP, g, split_at["v", i - 2] if i >= 2 else split_at["v", i + 2] - N_SP))
                sp.dma_start(raw_v[:, i % 2, :], wv0[g + 1, i]).then_inc(s_raw_v[i % 2], 16)

            for part in range(2):
                for twice in range(2):
                    sp.dma_start(M.k1_dram[part, :, twice, :, :], M.k1_rows[part]).then_inc(s_ktwice, 16)
            sp.sem_inc(s_raw_qk[0], 16)
            for i in range(2):
                sp.sem_inc(s_raw_v[i], 16 * (KT // 2))
            sp.dma_start(nraw[:, GH - 1, 0:NFTAIL], nf4_src[:, tail]).then_inc(s_tin, 16)
            with sp.Fori(0, GROUPS) as g:
                load_qk(g, 1)
                load_o(g, 0)
                load_o(g, 1)
                sp.wait_ge(s_biased, nth(2 * GH, g, -1))
                sp.dma_start(bias_sb[:, :, :], pbias[g]).then_inc(s_bias, 16)
                load_qk(g, 2)
                load_v(g, 0)
                load_v(g, 1)
                load_qk(g, 3)
                load_o(g, 2)
                load_o(g, 3)
                load_qk(g, GH)
                load_v(g, 2)
                load_v(g, 3)
            sp.wait_ge(s_ktwice, 16 * 4)

        @block.gpsimd
        def _(pool):
            def split(g, m, i):
                dst, low, src, arrived = piece(m, i)
                if m == "v":
                    reader, count = pj_at["v", 0, NB - 1], (g + 1) * 32 + 16 * (i // 2 + 1)
                elif m == "o":
                    reader, count = (pj_at["o", 0, NB - 1] if i >= 2 else -1), g * 32 + 16 * (i // 2 + 1)
                else:
                    reader, count = (pj_at[m, i - 1, 1] if i > 1 else pj_at[m, GH, 1] - N_PJ), g * 32 + 16 * (i // 2 + 1)
                pool.wait_ge(s_pj, nth(N_PJ, g, reader))
                pool.wait_ge(arrived, count)
                pool.sem_inc(s_turn, 1)
                pool.tensor_copy(dst, src).then_inc(s_whi, 1)
                pool.wait_ge(s_whi, nth(N_SP, g, split_at[m, i]))
                pool.sem_inc(s_turn, 1)
                pool.tensor_tensor(low, src, dst, ALU.subtract).then_inc(s_wlo, 1)

            def load_nf4(g, c):
                pool.wait_ge(s_nout[c], nth(16, g, -1))
                pool.dma_start(nraw[:, c, :], nf4_src[:, bass.ts(g * GH + c, NFC)]).then_inc(s_nin[c], 16)

            pool.sem_inc(s_whi, N_SP)
            pool.sem_inc(s_wlo, N_SP)
            with pool.Fori(0, GROUPS) as g:
                for n, (m, i) in enumerate(SPLITS):
                    if n < GH:
                        load_nf4(g, n)
                    split(g, m, i)

        @block.scalar
        def _(act):
            act.sem_inc(s_ev, N_EV - 4)
            act.sem_inc(s_nsign, N_NF)
            for s in (s_exp, s_pTc, s_ahi):
                act.sem_inc(s, 2 * GH)
            for c in range(GH - 1):
                act.sem_inc(s_nout[c], 16)

            def evacuate(m, h, j, g):
                n = pj_at[m, h, j]
                act.wait_ge(s_pj, nth(N_PJ, g, n))
                dst = V[:, j, :] if m == "v" else (qT if m == "q" else kT)[:, half(j)]
                act.activation(dst, M.pj[n % 4][:, :], ACT.Copy).then_inc(s_ev, 1)

            for m in "qk":
                for j in range(2):
                    evacuate(m, GH, j, -1)
            act.wait_ge(s_tchain, 4)
            for k in range(NLEV):
                if k >= 4:
                    act.wait_ge(s_tlev, k - 3)
                act.activation(nsign[:, k % 4, 0:NFTAIL], nnorm[:, 1, 0:NFTAIL], ACT.Sign,
                               bias=-nf4_threshold(k)).then_inc(s_tsign, 1)
            act.wait_ge(s_tlev, NLEV + 1)
            act.dma_start(M.nf4_dq[:, tail], nraw[:, GH - 1, 0:NFTAIL]).then_inc(s_nout[GH - 1], 16)
            with act.Fori(0, GROUPS) as g:
                level = [0]

                def nf4_out(c):
                    act.wait_ge(s_ndq, nth(GH, g, c))
                    act.dma_start(M.nf4_dq[:, bass.ts(g * GH + c, NFC)], nraw[:, c, :]).then_inc(s_nout[c], 16)

                def nf4_signs(n):
                    for k in range(level[0], level[0] + n):
                        c, lev = divmod(k, NLEV)
                        if lev == 5 and c:
                            nf4_out(c - 1)
                        if lev == 0:
                            act.wait_ge(s_nprep, nth(4 * GH, g, 4 * c + 3))
                        act.wait_ge(s_nlev, nth(N_NF, g, k - 4))
                        act.activation(nsign[:, k % 4, :], nnorm[:, c % 2, :], ACT.Sign,
                                       bias=-nf4_threshold(lev)).then_inc(s_nsign, 1)
                    level[0] += n

                def exps(h):
                    for j in range(2):
                        act.wait_ge(s_max, nth(2 * GH, g, 2 * h + j))
                        for b in range(QUAD * j, QUAD * (j + 1)):
                            e = act.activation(prob[:, h % 2, tile(b)], prob[:, h % 2, tile(b)], ACT.Exp,
                                               bias=nmax[:, h % 2, b:b + 1], accum_out=rsum[:, h % 2, b:b + 1])
                        e.then_inc(s_exp, 1)

                def copy_probT(h):
                    for j in range(2):
                        act.wait_ge(s_pT, nth(2 * GH, g, 2 * h + j))
                        act.activation(probT[:, half(j)], M.tp[j][:, :], ACT.Copy).then_inc(s_pTc, 1)

                def attn_high(h):
                    for j in range(2):
                        act.wait_ge(s_pv, nth(2 * GH, g, 2 * h + j))
                        act.activation(a_hi[:, slot(h), half(j)], M.tp[j][:, :], ACT.Copy).then_inc(s_ahi, 1)

                evacuate("v", 0, 0, g)
                exps(0)
                evacuate("v", 0, 1, g)
                nf4_signs(2)
                for b in range(2, NB):
                    evacuate("v", 0, b, g)
                    nf4_signs(4 if b < 6 else 3)
                for h in (1, 2, 3):
                    if h > 1:
                        exps(h - 1)
                    evacuate("q", h, 0, g)
                    evacuate("q", h, 1, g)
                    nf4_signs(0 if h == 1 else 1)
                    evacuate("k", h, 0, g)
                    copy_probT(h - 1)
                    nf4_signs(2)
                    evacuate("k", h, 1, g)
                    nf4_signs(2 if h == 1 else 0)
                    attn_high(h - 1)
                    nf4_signs(4)
                exps(3)
                nf4_signs(1)
                evacuate("q", GH, 0, g)
                nf4_signs(2)
                evacuate("q", GH, 1, g)
                nf4_signs(1)
                copy_probT(3)
                evacuate("k", GH, 0, g)
                nf4_signs(1)
                attn_high(3)
                evacuate("k", GH, 1, g)
                nf4_signs(N_NF - level[0])
                nf4_out(GH - 1)
            for c in range(GH):
                act.wait_ge(s_nout[c], 16 * (GROUPS + 1))

        @block.vector
        def _(dve):
            for s, n in ((s_oadd, N_O), (s_biased, 2 * GH), (s_max, 2 * GH), (s_prob, 2 * GH),
                         (s_alo, 2 * GH), (s_nprep, 4 * GH), (s_nlev, N_NF), (s_ndq, GH), (s_rsum, 4 * GH)):
                dve.sem_inc(s, n)

            dve.wait_ge(s_tin, 16)
            raw, norm, code = nraw[:, GH - 1, 0:NFTAIL], nnorm[:, 1, 0:NFTAIL], ncode[:, 0:NFTAIL]
            nf4_prepare(dve, s_tchain, lambda n: n + 1, raw, norm, nabs[:, 1, :], nrec, NFTAIL)
            for k in range(NLEV):
                dve.wait_ge(s_tsign, k + 1)
                if k:
                    dve.wait_ge(s_tlev, k)
                nf4_level(dve, k, nsign[:, k % 4, 0:NFTAIL], code).then_inc(s_tlev, 1)
            dve.wait_ge(s_tlev, NLEV)
            nf4_finish(dve, raw, code, nabs[:, 1, :], NFTAIL).then_inc(s_tlev, 1)
            dve.wait_ge(s_tlev, NLEV + 1)
            with dve.Fori(0, GROUPS) as g:
                level = [0]

                def nf4_begin(c):
                    dve.wait_ge(s_nin[c], g * 16 + 16)
                    nf4_prepare(dve, s_nprep, lambda n: nth(4 * GH, g, 4 * c + n), nraw[:, c, :], nnorm[:, c % 2, :],
                                nabs[:, c % 2, :], nrec, NFC)

                def nf4_levels(n):
                    for k in range(level[0], level[0] + n):
                        c, lev = divmod(k, NLEV)
                        dve.wait_ge(s_nsign, nth(N_NF, g, k))
                        dve.wait_ge(s_nlev, nth(N_NF, g, k - 1))
                        if lev == 0:
                            dve.wait_ge(s_ndq, nth(GH, g, c - 1))
                        nf4_level(dve, lev, nsign[:, k % 4, :], ncode[:, :]).then_inc(s_nlev, 1)
                        if lev == NLEV // 2 and c < GH - 1:
                            nf4_begin(c + 1)
                        if lev == NLEV - 1:
                            dve.wait_ge(s_nlev, nth(N_NF, g, k))
                            nf4_finish(dve, nraw[:, c, :], ncode, nabs[:, c % 2, :], NFC).then_inc(s_ndq, 1)
                    level[0] += n

                def bias_and_max(h):
                    for j in range(2):
                        part = prob[:, h % 2, half(j)].rearrange("p (b k) -> p b k", b=QUAD)
                        dve.wait_ge(s_score, nth(2 * GH, g, 2 * h + j))
                        dve.tensor_tensor(part, M.sc[j][:, :].rearrange("p (b k) -> p b k", b=QUAD),
                                          bias_sb[:, h:h + 1, :].broadcast_to([P, QUAD, S]), ALU.add).then_inc(s_biased, 1)
                        dve.wait_ge(s_biased, nth(2 * GH, g, 2 * h + j))
                        dve.tensor_reduce(nmax[:, h % 2, QUAD * j:QUAD * (j + 1)], part, AX.X, ALU.max,
                                          negate=True).then_inc(s_max, 1)

                def normalize(h):
                    for j in range(2):
                        sums = rsum[:, h % 2, QUAD * j:QUAD * (j + 1)]
                        dve.wait_ge(s_exp, nth(2 * GH, g, 2 * h + j))
                        dve.reciprocal(sums, sums).then_inc(s_rsum, 1)
                        dve.wait_ge(s_rsum, nth(4 * GH, g, 4 * h + 2 * j))
                        dve.tensor_tensor(sums, sums, M.rowany[:, QUAD * j:QUAD * (j + 1)], ALU.mult).then_inc(s_rsum, 1)
                        dve.wait_ge(s_rsum, nth(4 * GH, g, 4 * h + 2 * j + 1))
                        for b in range(QUAD * j, QUAD * (j + 1)):
                            last = dve.tensor_scalar(prob[:, h % 2, tile(b)], prob[:, h % 2, tile(b)],
                                                     rsum[:, h % 2, b:b + 1], None, ALU.mult)
                        last.then_inc(s_prob, 1)

                def attn_low(h):
                    for j in range(2):
                        dve.wait_ge(s_ahi, nth(2 * GH, g, 2 * h + j))
                        dve.tensor_tensor(a_lo[:, slot(h), half(j)], M.tp[j][:, :], a_hi[:, slot(h), half(j)],
                                          ALU.subtract).then_inc(s_alo, 1)

                def add_out(pair, t):
                    n = pj_at["o", pair, t]
                    dve.wait_ge(s_pj, nth(N_PJ, g, n))
                    dve.wait_ge(s_oadd, nth(N_O, g, o_at["o", pair, t] - NB))
                    dve.scalar_tensor_tensor(M.acc[:, t, :], M.pj[n % 4][:, :], M.tg[:, 0:1], M.acc[:, t, :],
                                             op0=ALU.mult, op1=ALU.add).then_inc(s_oadd, 1)

                dve.wait_ge(s_bias, g * 16 + 16)
                bias_and_max(0)
                nf4_begin(0)
                nf4_levels(2)
                normalize(0)
                nf4_levels(20)
                for h in (1, 2, 3):
                    if h > 1:
                        bias_and_max(h - 1)
                        normalize(h - 1)
                    nf4_levels(6 if h == 2 else 5)
                    attn_low(h - 1)
                    nf4_levels(2)
                bias_and_max(3)
                for t in range(4):
                    add_out(0, t)
                normalize(3)
                for t in range(4, NB):
                    add_out(0, t)
                    nf4_levels(1 if t < NB - 1 else 4)
                attn_low(3)
                for t in range(NB):
                    add_out(1, t)
                    nf4_levels(2 if t < 2 else 1 if t < NB - 1 else N_NF - level[0])

        @block.tensor
        def _(pe):
            pe.sem_inc(s_pj, PRIOR_PJ)
            pe.sem_inc(s_score, 2 * GH)
            pe.sem_inc(s_pT, 2 * GH)
            pe.sem_inc(s_pv, 2 * GH)
            def take(m, h, j, g):
                n = pj_at[m, h, j]
                was = PJ_USES[n - 4]
                if was[0] == "o":
                    pe.wait_ge(s_oadd, nth(N_O, g, o_at[was] - (0 if n >= 4 else N_O)))
                else:
                    pe.wait_ge(s_ev, nth(N_EV, g, ev_at[was]))
                return M.pj[n % 4]

            def three_pass(bank, w, wl, m, ml, first, last):
                pe.matmul(bank, w, m, start=first, stop=False)
                pe.matmul(bank, w, ml, start=False, stop=False)
                return pe.matmul(bank, wl, m, start=False, stop=last)

            def project(m, h, j, g):
                bank = take(m, h, j, g)
                if j == 0:
                    pe.wait_ge(s_wlo, nth(N_SP, g, split_at[m, h]))
                mi = "qk".index(m)
                hi, lo = (M.xT_hi, M.xT_lo) if m == "q" else (M.cT_hi, M.cT_lo)
                for k in range(KT):
                    w = slice(k * DH0, (k + 1) * DH0)
                    mm = three_pass(bank[:, :], qk_hi[:, mi, w], qk_lo[:, mi, w], hi[:, k, half(j)],
                                    lo[:, k, half(j)], k == 0, k == KT - 1)
                mm.then_inc(s_pj, 1)

            for m in "qk":
                for j in range(2):
                    project(m, GH, j, -1)
            pe.wait_ge(s_pj, PRIOR_PJ + 4)
            pe.sem_inc(s_pj, N_PJ - PRIOR_PJ - 4)
            with pe.Fori(0, GROUPS) as g:
                def values(b):
                    bank = take("v", 0, b, g)
                    for k in range(KT):
                        if b == 0:
                            pe.wait_ge(s_wlo, nth(N_SP, g, split_at["v", k] - N_SP))
                        mm = three_pass(bank[:, :], M.cT_hi[:, k, tile(b)], M.cT_lo[:, k, tile(b)], v_hi[:, k, :],
                                        v_lo[:, k, :], k == 0, k == KT - 1)
                    mm.then_inc(s_pj, 1)

                def scores(h):
                    pe.wait_ge(s_ev, nth(N_EV, g, ev_at["k", h, 1] if h else ev_at["k", GH, 1] - N_EV))
                    for j in range(2):
                        pe.wait_ge(s_biased, nth(2 * GH, g, 2 * h + j - 2))
                        pe.matmul(M.sc[j][:, :], M.ident_b[:, :], M.maskneg[:, half(j)], start=True, stop=False)
                        for b in range(QUAD * j, QUAD * (j + 1)):
                            mm = pe.matmul(M.sc[j][:, in_half(b)], qT[:, tile(b)], kT[:, tile(b)], start=False,
                                           stop=(b % QUAD == QUAD - 1))
                        mm.then_inc(s_score, 1)

                def transpose_probs(h):
                    for j in range(2):
                        pe.wait_ge(s_prob, nth(2 * GH, g, 2 * h + j))
                        pe.wait_ge(s_alo, nth(2 * GH, g, 2 * h + j - 2))
                        for b in range(QUAD * j, QUAD * (j + 1)):
                            mm = pe.transpose(M.tp[j][:, in_half(b)], prob[:, h % 2, tile(b)], M.ident[:, :])
                        mm.then_inc(s_pT, 1)

                def weigh_values(h):
                    for j in range(2):
                        pe.wait_ge(s_pTc, nth(2 * GH, g, 2 * h + j))
                        for b in range(QUAD * j, QUAD * (j + 1)):
                            mm = pe.matmul(M.tp[j][:, in_half(b)], V[:, b, h * DH0:(h + 1) * DH0], probT[:, tile(b)],
                                           start=True, stop=True)
                        mm.then_inc(s_pv, 1)

                def project_out(pair, t):
                    bank = take("o", pair, t, g)
                    if t == 0:
                        pe.wait_ge(s_wlo, nth(N_SP, g, split_at["o", 2 * pair + 1]))
                    pe.wait_ge(s_alo, nth(2 * GH, g, 2 * (2 * pair + 1) + t // QUAD))
                    for h in (2 * pair, 2 * pair + 1):
                        mm = three_pass(bank[:, :], a_hi[:, slot(h), tile(t)], a_lo[:, slot(h), tile(t)],
                                        o_hi[:, h % 2, :], o_lo[:, h % 2, :], h % 2 == 0, h % 2 == 1)
                    mm.then_inc(s_pj, 1)

                scores(0)
                for b in range(NB):
                    values(b)
                for h in (1, 2, 3):
                    project("q", h, 0, g)
                    project("q", h, 1, g)
                    project("k", h, 0, g)
                    transpose_probs(h - 1)
                    project("k", h, 1, g)
                    weigh_values(h - 1)
                    scores(h)
                for t in range(NB):
                    project_out(0, t)
                project("q", GH, 0, g)
                project("q", GH, 1, g)
                transpose_probs(3)
                project("k", GH, 0, g)
                weigh_values(3)
                project("k", GH, 1, g)
                for t in range(NB):
                    project_out(1, t)


def load_gptq(sp, tiles, arrived, gq, gs, gz, t, u):
    raw, scale, zwords = tiles
    sp.dma_start(raw[:, u, :], gq[t, u]).then_inc(arrived, 16)
    sp.dma_start(scale[:, u, :], gs[t, u].partition_broadcast(P)).then_inc(arrived, 16)
    sp.dma_start(zwords[:, u, :], gz[t, u].partition_broadcast(P)).then_inc(arrived, 16)


def attention1_phase(nc, M, sb, sem, wo1, gq, gs, gz, nibble_shift):
    W = REP1 * S
    UNITS = 2 * NB
    s_w_hi = sem("s_a1_w_hi")
    s_w_lo = sem("s_a1_w_lo")
    s_proj = sem("s_a1_proj")
    s_qhi = sem("s_a1_qhi")
    s_qlo = sem("s_a1_qlo")
    s_zero = sem("s_a1_zero")
    s_in = [sem(f"s_a1_in{i}") for i in range(2)]
    s_score = sem("s_a1_score")
    s_nmax = sem("s_a1_nmax")
    s_exp = sem("s_a1_exp")
    s_vzero = sem("s_a1_vzero")
    s_vin = sem("s_a1_vin")
    s_turn = sem("s_a1_turn")
    s_pT = sem("s_a1_pT")
    s_pTc = sem("s_a1_pTc")
    s_pv = sem("s_a1_pv")
    s_rsum = sem("s_a1_rsum")
    s_rec = sem("s_a1_rec")
    s_prob = sem("s_a1_prob")
    s_ahi = sem("s_a1_ahi")
    s_alo = sem("s_a1_alo")
    s_out, s_acc = (sem(f"s_a1_{n}") for n in ("out", "acc"))
    BAND = REP1 * DH1
    half = lambda j: slice(j * HALF, (j + 1) * HALF)
    tile = lambda b: slice(b * S, (b + 1) * S)

    with ExitStack() as local:
        w_hi = sb("w1_hi", [P, KT, D], F32R, local)
        w_lo = sb("w1_lo", [P, KT, D], F32R, local)
        q_hi = sb("q1_hi", [P, KT, TOK], F32R, local)
        q_lo = sb("q1_lo", [P, KT, TOK], F32R, local)
        k_hi = sb("k1d_hi", [P, 2, NB, REP1, S], F32R, local)
        k_lo = sb("k1d_lo", [P, 2, NB, REP1, S], F32R, local)
        qr = sb("qr", [P, 2, TOK], F32R, local)
        prob = sb("prob1", [P, 4, W], F32, local)
        probT = sb("probT1", [P, 2, W], F32, local)
        nmax = sb("nmax1", [P, 4, REP1], F32, local)
        rsum = sb("rsum1", [P, 4, REP1], F32, local)
        v_at = slice(P - DH1, P)
        vwin = sb("vwin", [P, 2, NB, P + BAND - DH1], F32, local)
        ln = TailNorm(M, sem, "f1_ln", prob[:, 0:2, :])
        block = local.enter_context(nc.Block())
        wo_steps = [2 * (k + 3) for k in range(KT)]
        DMAS = 4 * REP1

        @block.sync
        def _(sp):
            for k in range(KT):
                sp.wait_ge(s_w_lo, k + 1)
                sp.dma_start(M.w_raw[:, k, :], wo1[:, k, :]).then_inc(M.s_wraw[k], 16)
            with sp.Fori(0, KV1 // 2) as g:
                sp.wait_ge(s_qlo, g * 2 + 2)
                for par in range(2):
                    sp.wait_ge(s_zero, 2 * par + 2)
                    sp.wait_ge(s_score, nth(UNITS, g, par * NB + NB - 1 - UNITS))
                    for a in range(REP1):
                        rows = slice(32 * a, 32 * a + 32)
                        src = slice(64 * par + DH1 * a, 64 * par + DH1 * (a + 1))
                        for part, dst in enumerate((k_hi, k_lo)):
                            sp.dma_start(dst[rows, par, :, a, :].bitcast(F32),
                                         M.k1_dram[part, g * 2 + par].rearrange("c d (b k) -> (c d) b k", k=S)).then_inc(s_in[par], 16)
                        for part, s_src in enumerate((q_hi, q_lo)):
                            to = 32 * a + DH1 * part
                            sp.dma_start(qr[to:to + DH1, par, :].bitcast(F32), s_src[src, g, :].bitcast(F32)).then_inc(s_in[par], 16)
            sp.dma_start(M.shift[:, :], nibble_shift).then_inc(M.s_shift, 16)
            for u in range(3):
                load_gptq(sp, (M.raw_first, M.scale_first, M.zwords_first), M.s_first_in[u], gq, gs, gz, 0, u)

        @block.gpsimd
        def _(pool):
            pool.sem_inc(s_prob, UNITS)
            for par in range(2):
                for t in (k_hi, k_lo):
                    pool.memset(t[:, par, :, :, :].rearrange("p b a k -> p (b a k)").bitcast(F32), 0.0).then_inc(s_zero, 1)
                pool.memset(vwin[:, par, :, :], 0.0).then_inc(s_vzero, 1)

            def step(g, n, first=False):
                if n in (0, NB):
                    par = n // NB
                    pool.wait_ge(s_vzero, 2)
                    pool.wait_ge(s_pv, nth(UNITS, g, par * NB + NB - 1 - UNITS))
                    pool.sem_inc(s_turn, 1)
                    pool.tensor_copy(vwin[:, par, :, v_at],
                                     M.v1[:, :, bass.ds(g * 2 + par, 1), :].rearrange("p b j d -> p (b j) d")).then_inc(s_vin, 1)
                m = n - 1
                if m >= 0 or not first:
                    pool.wait_ge(s_rec, nth(UNITS, g, m))
                    p = prob[:, m % 4, :].rearrange("p (a k) -> p a k", a=REP1)
                    pool.tensor_tensor(p, p, rsum[:, m % 4, :].unsqueeze(2).broadcast_to([P, REP1, S]),
                                       ALU.mult).then_inc(s_prob, 1)

            pipelined(pool, KV1 // 2, UNITS, step, 1)

        @block.scalar
        def _(act):
            act.sem_inc(s_exp, UNITS)
            act.sem_inc(s_pTc, UNITS)
            act.sem_inc(s_ahi, 4)
            for k in range(KT):
                act.wait_ge(M.s_wraw[k], 16)
                act.activation(w_hi[:, k, :], M.w_raw[:, k, :], ACT.Copy).then_inc(s_w_hi, 1)
            for n in range(2 * KT):
                act.wait_ge(s_proj, n + 1)
                act.activation(q_hi[:, n // 2, half(n % 2)], M.pj[n % 4][:, :], ACT.Copy, scale=DH1 ** -0.5).then_inc(s_qhi, 1)
            def step(g, n, first=False):
                if first and n in wo_steps:
                    k = wo_steps.index(n)
                    act.wait_ge(M.s_wraw[k], 32)
                    act.activation(w_hi[:, k, :], M.w_raw[:, k, :], ACT.Copy).then_inc(s_w_hi, 1)
                m = n - 3
                if (m >= 0 or not first) and m < UNITS:
                    act.wait_ge(s_pT, nth(UNITS, g, m))
                    act.wait_ge(s_pv, nth(UNITS, g, m - 2))
                    act.activation(probT[:, m % 2, :], M.tp[m % 2][:, :], ACT.Copy).then_inc(s_pTc, 1)
                if n < UNITS:
                    act.wait_ge(s_nmax, nth(UNITS, g, n))
                    act.wait_ge(s_pT, nth(UNITS, g, n - 4))
                    for a in range(REP1):
                        last = act.activation(prob[:, n % 4, tile(a)], M.pj[n % 4][:, tile(a)], ACT.Exp,
                                              bias=nmax[:, n % 4, a:a + 1])
                    last.then_inc(s_exp, 1)
                m = n - 5
                if m % QUAD == QUAD - 1 and (m >= 0 or not first):
                    q, turn = (m // QUAD) % 4, g if m >= 0 else g - 1
                    rows = slice(BAND * (q // 2), BAND * (q // 2 + 1))
                    act.wait_ge(s_pv, nth(UNITS, g, m))
                    act.activation(M.xT_hi[rows, bass.ds(turn, 1), half(q % 2)].rearrange("p j s -> p (j s)"),
                                   M.sc[q % 2][rows, :], ACT.Copy).then_inc(s_ahi, 1)

            pipelined(act, KV1 // 2, UNITS, step, 5)
            for b in range(NB + 2):
                if b < NB:
                    ln.root(act, b)
                if b >= 2:
                    ln.high(act, b - 2)

        @block.vector
        def _(dve):
            for s, n in ((s_nmax, UNITS), (s_rec, UNITS), (s_rsum, UNITS), (s_alo, 4)):
                dve.sem_inc(s, n)
            def split_w(k, n):
                dve.wait_ge(s_w_hi, n)
                dve.tensor_tensor(w_lo[:, k, :], M.w_raw[:, k, :], w_hi[:, k, :], ALU.subtract).then_inc(s_w_lo, 1)

            for k in range(KT):
                split_w(k, k + 1)
            for n in range(2 * KT):
                dve.wait_ge(s_qhi, n + 1)
                dve.scalar_tensor_tensor(q_lo[:, n // 2, half(n % 2)], M.pj[n % 4][:, :], DH1 ** -0.5,
                                         q_hi[:, n // 2, half(n % 2)], op0=ALU.mult, op1=ALU.subtract).then_inc(s_qlo, 1)

            def step(g, n, first=False):
                if first and n in wo_steps:
                    split_w(wo_steps.index(n), KT + wo_steps.index(n) + 1)
                if n < UNITS:
                    dve.wait_ge(s_score, nth(UNITS, g, n))
                    scores = M.pj[n % 4][:, :].rearrange("p (a k) -> p a k", a=REP1)
                    dve.tensor_reduce(nmax[:, n % 4, :], scores, AX.X, ALU.max, negate=True).then_inc(s_nmax, 1)
                m = n - 1
                if (m >= 0 or not first) and m < UNITS:
                    sums = rsum[:, m % 4, :]
                    dve.wait_ge(s_exp, nth(UNITS, g, m))
                    dve.wait_ge(s_prob, nth(UNITS, g, m - 4))
                    dve.tensor_reduce(sums, prob[:, m % 4, :].rearrange("p (a k) -> p a k", a=REP1), AX.X,
                                      ALU.add).then_inc(s_rsum, 1)
                    dve.wait_ge(s_rsum, nth(UNITS, g, m))
                    dve.reciprocal(sums, sums).then_inc(s_rec, 1)
                m = n - 6
                if m % QUAD == QUAD - 1 and (m >= 0 or not first):
                    q, turn = (m // QUAD) % 4, g if m >= 0 else g - 1
                    at = (slice(BAND * (q // 2), BAND * (q // 2 + 1)), bass.ds(turn, 1), half(q % 2))
                    dve.wait_ge(s_ahi, nth(4, g, m // QUAD))
                    dve.tensor_tensor(M.xT_lo[at].rearrange("p j s -> p (j s)"), M.sc[q % 2][at[0], :],
                                      M.xT_hi[at].rearrange("p j s -> p (j s)"), ALU.subtract).then_inc(s_alo, 1)

            pipelined(dve, KV1 // 2, UNITS, step, 6)

            for b in range(NB + 2):
                if b < NB:
                    dve.wait_ge(s_out, b + 1)
                    dve.scalar_tensor_tensor(M.acc[:, b, :], M.pj[b % 4][:, :], M.tg[:, 1:2], M.acc[:, b, :],
                                             op0=ALU.mult, op1=ALU.add).then_inc(s_acc, 1)
                    dve.wait_ge(s_acc, b + 1)
                    ln.take_stats(dve, b)
                if 1 <= b <= NB:
                    ln.normalize(dve, b - 1)
                if b >= 2:
                    ln.low(dve, b - 2)

        @block.tensor
        def _(pe):
            pe.sem_inc(s_score, UNITS)
            pe.sem_inc(s_pT, UNITS)
            pe.sem_inc(s_pv, UNITS)
            for n in range(2 * KT):
                t, j = divmod(n, 2)
                if n >= 4:
                    pe.wait_ge(s_qlo, n - 3)
                for k in range(KT):
                    if n == 0:
                        pe.wait_ge(s_w_lo, k + 1)
                    hi, lo = w_hi[:, k, t * P:(t + 1) * P], w_lo[:, k, t * P:(t + 1) * P]
                    bank = M.pj[n % 4][:, :]
                    pe.matmul(bank, hi, M.xT_hi[:, k, half(j)], start=(k == 0), stop=False)
                    pe.matmul(bank, hi, M.xT_lo[:, k, half(j)], start=False, stop=False)
                    mm = pe.matmul(bank, lo, M.xT_hi[:, k, half(j)], start=False, stop=(k == KT - 1))
                mm.then_inc(s_proj, 1)
            pe.wait_ge(s_qlo, 2 * KT)

            def step(g, n, first=False):
                if n < UNITS:
                    par, b = divmod(n, NB)
                    if b == 0:
                        pe.wait_ge(s_in[par], g * (16 * DMAS) + 16 * DMAS)
                    pe.wait_ge(s_exp, nth(UNITS, g, n - 4))
                    pe.matmul(M.pj[n % 4][:, :], qr[:, par, tile(b)], k_hi[:, par, b, :, :], start=True, stop=False)
                    pe.matmul(M.pj[n % 4][:, :], qr[:, par, tile(b)], k_lo[:, par, b, :, :], start=False,
                              stop=True).then_inc(s_score, 1)
                m = n - 3
                if (m >= 0 or not first) and m < UNITS:
                    pe.wait_ge(s_prob, nth(UNITS, g, m))
                    pe.wait_ge(s_pTc, nth(UNITS, g, m - 2))
                    for a in range(REP1):
                        mm = pe.transpose(M.tp[m % 2][:, tile(a)], prob[:, m % 4, tile(a)], M.ident[:, :])
                    mm.then_inc(s_pT, 1)
                m = n - 4
                if m >= 0 or not first:
                    par, b = divmod(m % UNITS, NB)
                    pe.wait_ge(s_pTc, nth(UNITS, g, m))
                    if m % QUAD == 0:
                        pe.wait_ge(s_alo, nth(4, g, m // QUAD - 2))
                    if b == 0:
                        pe.wait_ge(s_vin, g * 2 + (par + 1 if m >= 0 else par - 1))
                    for a in range(REP1):
                        at = BAND * par + DH1 * a
                        rows = BAND * (par + 1)
                        window = slice(P - DH1 - at, P - DH1 - at + rows)
                        mm = pe.matmul(M.sc[(m // QUAD) % 2][0:rows, tile(m % QUAD)], vwin[:, par, b, window],
                                       probT[:, m % 2, tile(a)], start=(a == 0), stop=(a == REP1 - 1))
                    mm.then_inc(s_pv, 1)

            pipelined(pe, KV1 // 2, UNITS, step, 4)
            pe.wait_ge(s_alo, 4 + KV1 * 2)
            pe.wait_ge(s_w_lo, 2 * KT)
            for b in range(NB + 2):
                if b < NB:
                    if b >= 4:
                        pe.wait_ge(s_acc, b - 3)
                    bank = M.pj[b % 4][:, :]
                    for k in range(KT):
                        pe.matmul(bank, M.xT_hi[:, k, tile(b)], w_hi[:, k, :], start=(k == 0), stop=False)
                        pe.matmul(bank, M.xT_hi[:, k, tile(b)], w_lo[:, k, :], start=False, stop=False)
                        mm = pe.matmul(bank, M.xT_lo[:, k, tile(b)], w_hi[:, k, :], start=False, stop=(k == KT - 1))
                    mm.then_inc(s_out, 1)
                if b >= 2:
                    ln.transpose(pe, b - 2)


def pipelined(eng, turns, steps, step, drain):
    for n in range(steps):
        step(0, n, first=True)
    with eng.Fori(1, turns) as g:
        for n in range(steps):
            step(g, n)
    for n in range(steps, steps + drain):
        step(turns - 1, n, first=True)


class LayerNorm:

    def __init__(self, M, sem, tag, xn):
        self.M, self.xn = M, xn
        self.s_stats, self.s_xn, self.s_tr, self.s_hi, self.s_lo = (
            sem(f"s_{tag}_{n}") for n in ("stats", "xn", "transposed", "hi", "lo"))
        self.root = RootSteps(M, sem, tag)

    def take_stats(self, dve):
        layernorm_stats(dve, self.M, self.s_stats, self.root)

    def vector(self, dve):
        M = self.M
        self.root.vector(dve)
        for b in range(NB):
            dve.tensor_scalar(self.xn[:, b, :], M.acc[:, b, :], M.mv[:, b, 0:1], M.rs[:, b:b + 1],
                              ALU.subtract, ALU.mult).then_inc(self.s_xn, 1)
        for b in range(NB):
            at = slice(b * S, (b + 1) * S)
            dve.wait_ge(self.s_hi, b + 1)
            dve.tensor_tensor(M.xT_lo[:, :, at], M.pj[b % 4][:, :].rearrange("p (k s) -> p k s", k=KT),
                              M.xT_hi[:, :, at], ALU.subtract).then_inc(self.s_lo, 1)

    def scalar(self, act):
        M = self.M
        self.root.scalar(act)
        for b in range(NB):
            act.wait_ge(self.s_tr, b + 1)
            act.activation(M.xT_hi[:, :, b * S:(b + 1) * S], M.pj[b % 4][:, :].rearrange("p (k s) -> p k s", k=KT),
                           ACT.Copy).then_inc(self.s_hi, 1)

    def tensor(self, pe):
        M = self.M
        for b in range(NB):
            pe.wait_ge(self.s_xn, b + 1)
            if b >= 4:
                pe.wait_ge(self.s_lo, b - 3)
            for k in range(KT):
                mm = pe.transpose(M.pj[b % 4][:, k * P:(k + 1) * P], self.xn[:, b, k * P:(k + 1) * P], M.ident[:, :])
            mm.then_inc(self.s_tr, 1)


class TailNorm:

    def __init__(self, M, sem, tag, xn):
        self.M, self.xn, self.links = M, xn, 0
        self.s_chain, self.s_ve, self.s_root, self.s_xn, self.s_tr, self.s_hi, self.s_lo = (
            sem(f"s_{tag}_{n}") for n in ("chain", "ve", "root", "xn", "transposed", "hi", "lo"))

    def link(self, dve, instruction):
        self.links += 1
        instruction.then_inc(self.s_chain, 1)
        dve.wait_ge(self.s_chain, self.links)

    def take_stats(self, dve, b):
        M = self.M
        self.link(dve, dve.bn_stats(M.stats[:, b, :], M.acc[:, b, :]))
        self.link(dve, dve.bn_aggr(M.mv[:, b, :], M.stats[:, b, :]))
        dve.tensor_scalar(M.ve[:, b:b + 1], M.mv[:, b, 1:2], EPS, None, ALU.add).then_inc(self.s_ve, 1)

    def root(self, act, b):
        M = self.M
        act.wait_ge(self.s_ve, b + 1)
        act.activation(M.sd[:, b:b + 1], M.ve[:, b:b + 1], ACT.Sqrt).then_inc(self.s_root, 1)

    def normalize(self, dve, b):
        M = self.M
        ve, sd, rs, nt = (t[:, b:b + 1] for t in (M.ve, M.sd, M.rs, M.nt))
        dve.wait_ge(self.s_root, b + 1)
        self.link(dve, dve.reciprocal(rs, sd))
        self.link(dve, dve.scalar_tensor_tensor(nt, rs, ve, rs, op0=ALU.mult, op1=ALU.mult))
        self.link(dve, dve.tensor_scalar(nt, nt, -0.5, 1.5, ALU.mult, ALU.add))
        self.link(dve, dve.tensor_tensor(rs, rs, nt, ALU.mult))
        if b >= 2:
            dve.wait_ge(self.s_tr, b - 1)
        dve.tensor_scalar(self.xn[:, b % 2, :], M.acc[:, b, :], M.mv[:, b, 0:1], rs, ALU.subtract,
                          ALU.mult).then_inc(self.s_xn, 1)

    def transpose(self, pe, b):
        M = self.M
        pe.wait_ge(self.s_xn, b + 1)
        if b >= 2:
            pe.wait_ge(self.s_lo, b - 1)
        for k in range(KT):
            mm = pe.transpose(M.tp[b % 2][:, k * P:(k + 1) * P], self.xn[:, b % 2, k * P:(k + 1) * P], M.ident[:, :])
        mm.then_inc(self.s_tr, 1)

    def high(self, act, b):
        M = self.M
        act.wait_ge(self.s_tr, b + 1)
        act.activation(M.xT_hi[:, :, b * S:(b + 1) * S], M.tp[b % 2][:, :].rearrange("p (k s) -> p k s", k=KT),
                       ACT.Copy).then_inc(self.s_hi, 1)

    def low(self, dve, b):
        M = self.M
        at = slice(b * S, (b + 1) * S)
        dve.wait_ge(self.s_hi, b + 1)
        dve.tensor_tensor(M.xT_lo[:, :, at], M.tp[b % 2][:, :].rearrange("p (k s) -> p k s", k=KT),
                          M.xT_hi[:, :, at], ALU.subtract).then_inc(self.s_lo, 1)


def of_tile(per_tile, t, i):
    return (t + 2) * per_tile + (i + 1)


GATE, UP, DOWN = range(3)
LOOPED = FT - 3


def ffn_phase(nc, M, sb, sem, layer, wq1, gq=None, gs=None, gz=None, out=None):
    L = f"f{layer}"
    s_in = [M.s_first_in if layer and p == 0 else [sem(f"s_{L}_in{p}{u}") for u in range(3)] for p in range(2)]
    s_unit = sem(f"s_{L}_unit")
    s_hi = sem(f"s_{L}_hi")
    s_lo = sem(f"s_{L}_lo")
    s_gu = sem(f"s_{L}_gate_up")
    s_silu = sem(f"s_{L}_silu")
    s_h = sem(f"s_{L}_h")
    s_ints = sem(f"s_{L}_ints")
    s_hs_hi = sem(f"s_{L}_hs_hi")
    s_hs_lo = sem(f"s_{L}_hs_lo")
    s_down = sem(f"s_{L}_down")
    s_acc = sem(f"s_{L}_acc")
    s_zero = sem(f"s_{L}_zero")
    half = lambda j: slice(j * HALF, (j + 1) * HALF)
    tile = lambda b: slice(b * S, (b + 1) * S)
    gain = M.tg[:, 2 + layer:3 + layer]

    with ExitStack() as local:
        hT = sb(f"hT{layer}", [P, FT, TOK], F32, local)
        dn_hi = sb(f"dn_hi{layer}", [P, FT, D], F32R, local)
        dn_lo = sb(f"dn_lo{layer}", [P, FT, D], F32R, local)
        wT_hi = sb(f"wT_hi{layer}", [P, 2, 2, D], F32R, local)
        wT_lo = sb(f"wT_lo{layer}", [P, 2, 2, D], F32R, local)
        silu = sb(f"silu{layer}", [P, 2, HALF], F32, local)
        if layer == 0:
            raw = sb("raw0", [P, 2, 3, D], F32, local)
        else:
            raws = (M.raw_first, sb("raw1", [P, 3, D], I32, local))
            scales = (M.scale_first, sb("scale", [P, 3, D], F16, local))
            zwords = (M.zwords_first, sb("zwords", [P, 3, D // 8], I32, local))
            nibs = sb("nibs", [P, 2, D], I32, local)
            zeros = sb("zeros", [P, 2, D], I32, local)
            ints = sb("ints", [P, 2, D], F32, local)
            unit_f = sb("unit_f", [P, 2, D], F32, local)
            ffn_out = sb("ffn_out", [P, 2, D], F16, local)
        if layer == 0:
            s_out = None
            first = LayerNorm(M, sem, f"{L}_ln", hT[:, 0:NB * D // TOK, :].rearrange("p a (b d) -> p (a b) d", d=D))
            hs = [sb(f"hs_{n}", [P, 2, FT, S], F32R, local) for n in ("hi", "lo")]
            hs_hi, hs_lo = ([t[:, i, :, :] for i in range(2)] for t in hs)
            xn = sb("xn_f0", [P, 2, D], F32, local)
            ln = TailNorm(M, sem, "a1_ln", xn)
        else:
            s_out = sem("s_out")
            split_cols = FT * S
            flat = lambda t: t[:, :, :].rearrange("p k n -> p (k n)")
            hs_hi, hs_lo = ([flat(t)[:, i * split_cols:(i + 1) * split_cols].rearrange("p (f s) -> p f s", s=S)
                             for i in range(2)] for t in (M.xT_hi, M.xT_lo))
        block = local.enter_context(nc.Block())

        def over_tiles(eng, prepare, consume, between=None, both=None):
            if both is None:
                def both(ahead, ahead_par, t, par):
                    prepare(ahead, ahead_par)
                    consume(t, par)

            prepare(0, 0)
            if between:
                between()
            with eng.Fori(0, LOOPED // 2) as g:
                for par in range(2):
                    both(g * 2 + (par + 1), (par + 1) % 2, g * 2 + par, par)
            for t in range(LOOPED, FT):
                if t + 1 < FT:
                    both(t + 1, (t + 1) % 2, t, t % 2)
                else:
                    consume(t, t % 2)

        pieces = (slice(0, FT // 2), slice(FT // 2, FT))
        last_tile = lambda t: isinstance(t, int) and t == FT - 1
        rows_of = lambda t, u: FREST if layer == 0 and u == DOWN and last_tile(t) else P
        banks = [M.tp[0], M.tp[1], M.sc[0]]

        if layer == 0:
            flat_dq = M.nf4_dq.rearrange("p n -> (p n)")
            w1, w2 = (flat_dq[i * FPAD * D:(i + 1) * FPAD * D].rearrange("(t p n) -> t p n", t=FT, n=D) for i in range(2))
            w3 = flat_dq[2 * FPAD * D:].rearrange("(k p n) -> p k n", k=KT, n=FF)

        @block.sync
        def _(sp):
            def load(t, par):
                for u in range(3):
                    if layer and isinstance(t, int) and t == 0:
                        continue
                    sp.wait_ge(s_unit, of_tile(3, t - 2, u))
                    if layer:
                        load_gptq(sp, (raws[par], scales[par], zwords[par]), s_in[par][u], gq, gs, gz, t, u)
                    elif u < DOWN:
                        sp.dma_start(raw[:, par, u, :], (w1, w2)[u][t]).then_inc(s_in[par][u], 16)
                    else:
                        n = rows_of(t, u)
                        at = slice(t * P, t * P + n) if isinstance(t, int) else bass.ts(t, P)
                        sp.dma_start(raw[:, par, u, :].rearrange("p (k h) -> p k h", k=KT)[:, :, 0:n],
                                     w3[:, :, at]).then_inc(s_in[par][u], 16)

            def load_wq():
                for k in range(KT):
                    sp.dma_start(M.w_raw[:, k, :], wq1[:, k, :]).then_inc(M.s_wraw[k], 16)

            over_tiles(sp, load, lambda t, par: None, None if layer else load_wq)
            if layer:
                for b in range(NB):
                    sp.wait_ge(s_acc, b + 1)
                    sp.dma_start(out[b], M.acc[:, b, :]).then_inc(s_out, 16)
                sp.wait_ge(s_out, 16 * NB)

        arrivals = 48 if layer else 16
        arrived = lambda t, par: (t - par) * (arrivals // 2) + arrivals

        @block.gpsimd
        def _(pool):
            if layer == 0:
                for t in (dn_hi, dn_lo):
                    pool.memset(t[FREST:P, FT - 1, :].bitcast(F32), 0.0).then_inc(s_zero, 1)
            if layer:
                pool.sem_inc(s_unit, 6)

                def scale_unit(t, par):
                    for u in range(3):
                        i = (par * 3 + u) % 2
                        pool.wait_ge(s_lo, of_tile(3, t, u - 2))
                        pool.wait_ge(s_ints, of_tile(9, t, 3 * u + 2))
                        pool.tensor_tensor(unit_f[:, i, :], ints[:, i, :], scales[par][:, u, :],
                                           ALU.mult).then_inc(s_unit, 1)

                over_tiles(pool, scale_unit, lambda t, par: None)

        @block.scalar
        def _(act):
            act.sem_inc(s_hi, 6)
            act.sem_inc(s_silu, 4)

            def high(t, par, units=range(3)):
                for u in units:
                    n = rows_of(t, u)
                    act.wait_ge(s_gu, of_tile(4, t - 2, 3))
                    act.wait_ge(s_unit, of_tile(3, t, u))
                    if u == DOWN:
                        dst = dn_hi[0:n, t, :]
                        src = unit_f[:, (par * 3 + u) % 2, :] if layer else banks[u][0:n, :]
                    else:
                        dst = wT_hi[:, par, u, :]
                        src = unit_f[:, (par * 3 + u) % 2, :] if layer else banks[u][:, :]
                    act.activation(dst, src, ACT.Copy).then_inc(s_hi, 1)

            def silus(t, par, halves=range(2)):
                for j in halves:
                    act.wait_ge(s_gu, of_tile(4, t, 2 * j))
                    act.activation(silu[:, j, :], M.pj[2 * j][:, :], ACT.Silu).then_inc(s_silu, 1)

            def high_and_silus(ahead, ahead_par, t, par):
                high(ahead, ahead_par, (GATE,))
                silus(t, par, (0,))
                high(ahead, ahead_par, (UP, DOWN))
                silus(t, par, (1,))

            if layer:
                over_tiles(act, high, silus, both=high_and_silus)
            else:
                over_tiles(act, high, silus, lambda: first.scalar(act))
            for b in range(NB + (0 if layer else 4)):
                if b < NB:
                    if b >= 2:
                        act.wait_ge(s_down, b - 1)
                    for f in pieces:
                        act.wait_ge(s_h, of_tile(2, FT - 1 if layer else f.stop - 1, 1))
                        act.activation(hs_hi[b % 2][:, f, :], hT[:, f, tile(b)], ACT.Copy).then_inc(s_hs_hi, 1)
                if not layer:
                    if 2 <= b < NB + 2:
                        ln.root(act, b - 2)
                    if 3 <= b < NB + 3:
                        ln.high(act, b - 3)

        @block.vector
        def _(dve):
            dve.sem_inc(s_lo, 6)
            dve.sem_inc(s_h, 4)
            dve.sem_inc(s_ints, 18)
            if layer == 0:
                first.take_stats(dve)

            def unpack(t, par, u):
                i = (par * 3 + u) % 2
                dve.wait_ge(s_in[par][u], arrived(t, par))
                dve.wait_ge(M.s_shift, 16)
                dve.wait_ge(s_ints, of_tile(9, t, 3 * (u - 2) + 2))
                dve.tensor_scalar(nibs[:, i, :], raws[par][:, u, :], M.shift[:, 0:1], 15, ALU.logical_shift_right,
                                  ALU.bitwise_and).then_inc(s_ints, 1)
                z = zeros[:, i, :].rearrange("p (n e) -> p n e", e=8)
                for e in range(8):
                    last = dve.tensor_scalar(z[:, :, e], zwords[par][:, u, :], 4 * e, 15, ALU.logical_shift_right,
                                             ALU.bitwise_and)
                last.then_inc(s_ints, 1)
                dve.wait_ge(s_unit, of_tile(3, t, u - 2))
                dve.wait_ge(s_ints, of_tile(9, t, 3 * u + 1))
                dve.scalar_tensor_tensor(ints[:, i, :], nibs[:, i, :], 1.0, zeros[:, i, :], op0=ALU.subtract,
                                         op1=ALU.subtract).then_inc(s_ints, 1)

            def low(t, par, u):
                n = rows_of(t, u)
                dve.wait_ge(s_hi, of_tile(3, t, u))
                src = unit_f[0:n, (par * 3 + u) % 2, :] if layer else banks[u][0:n, :]
                hi = dn_hi[0:n, t, :] if u == DOWN else wT_hi[:, par, u, :]
                lo = dn_lo[0:n, t, :] if u == DOWN else wT_lo[:, par, u, :]
                dve.tensor_tensor(lo, src, hi, ALU.subtract).then_inc(s_lo, 1)

            def prepare(t, par):
                if layer:
                    unpack(t, par, GATE)
                    unpack(t, par, UP)
                    low(t, par, GATE)
                    unpack(t, par, DOWN)
                    low(t, par, UP)
                    low(t, par, DOWN)
                else:
                    for u in range(3):
                        low(t, par, u)

            def hidden(t, par, halves=range(2)):
                for j in halves:
                    dve.wait_ge(s_silu, of_tile(2, t, j))
                    dve.wait_ge(s_gu, of_tile(4, t, 2 * j + 1))
                    dve.tensor_tensor(hT[:, t, half(j)], M.pj[2 * j + 1][:, :], silu[:, j, :],
                                      ALU.mult).then_inc(s_h, 1)

            def unpack_and_hidden(ahead, ahead_par, t, par):
                unpack(ahead, ahead_par, GATE)
                unpack(ahead, ahead_par, UP)
                low(ahead, ahead_par, GATE)
                hidden(t, par, (0,))
                unpack(ahead, ahead_par, DOWN)
                low(ahead, ahead_par, UP)
                low(ahead, ahead_par, DOWN)
                hidden(t, par, (1,))

            if layer:
                over_tiles(dve, prepare, hidden, both=unpack_and_hidden)
            else:
                over_tiles(dve, prepare, hidden, lambda: first.vector(dve))

            def split(b):
                for i, f in enumerate(pieces):
                    dve.wait_ge(s_hs_hi, 2 * b + i + 1)
                    dve.tensor_tensor(hs_lo[b % 2][:, f, :], hT[:, f, tile(b)], hs_hi[b % 2][:, f, :],
                                      ALU.subtract).then_inc(s_hs_lo, 1)

            for b in range(NB + (2 if layer else 3)):
                if b < NB:
                    split(b)
                c = b - 2
                if 0 <= c < NB:
                    dve.wait_ge(s_down, c + 1)
                    y = M.pj[c % 4][:, :]
                    if layer:
                        dve.tensor_copy(ffn_out[:, c % 2, :], y).then_inc(s_zero, 1)
                        dve.wait_ge(s_zero, c + 1)
                        y = ffn_out[:, c % 2, :]
                    dve.scalar_tensor_tensor(M.acc[:, c, :], y, gain, M.acc[:, c, :], op0=ALU.mult,
                                             op1=ALU.add).then_inc(s_acc, 1)
                    if not layer:
                        dve.wait_ge(s_acc, c + 1)
                        ln.take_stats(dve, c)
                if not layer:
                    if c >= 1:
                        ln.low(dve, c - 1)
                    if 0 <= c < NB:
                        ln.normalize(dve, c)
            dve.wait_ge(s_acc, NB)

        @block.tensor
        def _(pe):
            pe.sem_inc(s_gu, 8)
            if layer == 0:
                pe.sem_inc(s_unit, 6)

            def transposes(t, par):
                if layer:
                    return
                for u in range(3):
                    n = rows_of(t, u)
                    pe.wait_ge(s_in[par][u], arrived(t, par))
                    pe.wait_ge(s_lo, of_tile(3, t - 1, u))
                    for k in range(KT):
                        mm = pe.transpose(banks[u][0:n, k * P:(k + 1) * P], raw[:, par, u, k * P:k * P + n],
                                          M.ident[:, :])
                    mm.then_inc(s_unit, 1)

            def products(t, par):
                for j in range(2):
                    for u in (GATE, UP):
                        bank = M.pj[2 * j + u][:, :]
                        pe.wait_ge(s_h, of_tile(2, t - 1, j))
                        if layer == 0 and par == 0:
                            pe.wait_ge(first.s_lo, QUAD + 1 + u if j == 0 else NB)
                        if j == 0:
                            pe.wait_ge(s_lo, of_tile(3, t, u))
                        for k in range(KT):
                            w = slice(k * P, (k + 1) * P)
                            hi, lo = wT_hi[:, par, u, w], wT_lo[:, par, u, w]
                            pe.matmul(bank, hi, M.xT_hi[:, k, half(j)], start=(k == 0), stop=False)
                            pe.matmul(bank, hi, M.xT_lo[:, k, half(j)], start=False, stop=False)
                            mm = pe.matmul(bank, lo, M.xT_hi[:, k, half(j)], start=False, stop=(k == KT - 1))
                        mm.then_inc(s_gu, 1)

            over_tiles(pe, transposes, products, None if layer else lambda: first.tensor(pe))
            for b in range(NB + (0 if layer else 1)):
                if b == NB:
                    ln.transpose(pe, b - 1)
                    break
                bank = M.pj[b % 4][:, :]
                if b == 0:
                    pe.wait_ge(s_lo, of_tile(3, FT - 1, DOWN))
                    if layer == 0:
                        pe.wait_ge(s_zero, 2)
                if b >= 4:
                    pe.wait_ge(s_acc, b - 3)
                for t in range(FT):
                    for i, f in enumerate(pieces):
                        if t == f.start:
                            pe.wait_ge(s_hs_lo, 2 * b + i + 1)
                    pe.matmul(bank, hs_hi[b % 2][:, t, :], dn_hi[:, t, :], start=(t == 0), stop=False)
                    pe.matmul(bank, hs_hi[b % 2][:, t, :], dn_lo[:, t, :], start=False, stop=False)
                    mm = pe.matmul(bank, hs_lo[b % 2][:, t, :], dn_hi[:, t, :], start=False, stop=(t == FT - 1))
                mm.then_inc(s_down, 1)
                if layer == 0 and b:
                    ln.transpose(pe, b - 1)


_OUT = ((NB, S, D), "float32")


def kernel(**inputs):
    import concourse.bacc as bacc
    from concourse.bass_utils import run_bass_kernel_spmd

    a = {k: np.asarray(v) for k, v in inputs.items()}
    by_head = lambda w: w.reshape(H0, DH0, KT, P).transpose(0, 3, 2, 1)
    pad = ((0, FPAD - FF), (0, 0))
    nf4 = np.concatenate([np.pad(a["L0_ffn_w1"], pad).reshape(-1), np.pad(a["L0_ffn_w2"], pad).reshape(-1),
                          a["L0_ffn_w3"].reshape(-1)])

    g = {k[7:]: v for k, v in a.items() if k.startswith("L1_ffn_")}
    padded = lambda w, rows, cols: np.pad(w, ((0, rows - w.shape[0]), (0, cols - w.shape[1])))
    by_tile = lambda w: np.moveaxis(w.reshape(*w.shape[:-1], FT, -1), -2, 0)
    across = lambda w: by_tile(w).reshape(FT, -1)
    words = lambda w, rows, cols: np.repeat(padded(w, rows // 8, cols), 8, axis=0)
    wide = lambda w: by_tile(words(w, D, FPAD).reshape(KT, P, FPAD).transpose(1, 0, 2)).reshape(FT, P, D)
    gq = np.stack([wide(g["gate_qweight"]), wide(g["up_qweight"]),
                   words(g["down_qweight"], FPAD, D).reshape(FT, P, D)], 1)
    gs = np.stack([across(padded(g["gate_scales"], KT, FPAD)), across(padded(g["up_scales"], KT, FPAD)),
                   g["down_scales"]], 1)
    gz = np.stack([across(padded(g["gate_zeros"], KT, FPAD // 8)), across(padded(g["up_zeros"], KT, FPAD // 8)),
                   g["down_zeros"]], 1)
    arrays = {
        "x": a["x"], "ctx_in": a["ctx_4096"],
        "mask": np.ascontiguousarray(a["mask_BxSxS2_bk0"]).view(np.int32),
        "gains": np.concatenate([a["g_xattn"], a["g_ffn"]]), "lnw": a["L0_xattn_ln_weight"],
        "pbias": a["L0_xattn_position_bias"].reshape(GROUPS, GH, S, S).transpose(0, 2, 1, 3),
        "wqk0": np.pad(np.stack([by_head(a["L0_xattn_w_q"]), by_head(a["L0_xattn_w_k"])], 2)
                       .reshape(H0, P, 2 * KT * DH0), ((0, 1), (0, 0), (0, 0))),
        "wv0": np.pad(a["L0_xattn_w_v"].reshape(GROUPS, GH * DH0, KT, P).transpose(0, 2, 3, 1),
                      ((0, 1), (0, 0), (0, 0), (0, 0))),
        "wo0": a["L0_xattn_w_out"].T.reshape(H0, P, D),
        "nf4_src": nf4.reshape(P, NFW), "gq": gq, "gs": gs, "gz": gz,
        "wkv1": np.stack([a[f"L1_xattn_W{m}"].reshape(KT, P, P).transpose(1, 0, 2).reshape(P, KT * P) for m in "kv"], 1),
        "wq1": a["L1_xattn_Wq"].reshape(KT, P, D).transpose(1, 0, 2), "wo1": a["L1_xattn_Wo"].reshape(KT, P, D).transpose(1, 0, 2),
        "nibble_shift": (4 * (np.arange(P, dtype=np.int32) % 8)).reshape(P, 1),
    }
    arrays = {k: np.ascontiguousarray(v) for k, v in arrays.items()}
    nc = bacc.Bacc("TRN2", target_bir_lowering=False, num_devices=1, dynamic_dma_scratch_size=8192)
    aps = {k: nc.dram_tensor(f"in_{k}", v.shape, mybir.dt.from_np(v.dtype), kind="ExternalInput").ap()
           for k, v in arrays.items()}
    out = nc.dram_tensor("out_dram", _OUT[0], F32, kind="ExternalOutput").ap()
    flamingo(nc, **aps, out=out)
    r = run_bass_kernel_spmd(nc, [{f"in_{k}": v for k, v in arrays.items()}], core_ids=[0])
    return r.results[0]["out_dram"]
```
